# Optimizing a Trainium2 kernel written in Bass

```python
import numpy as np
import jax
import jax.numpy as jnp

def _softmax(x, axis=-1):
    return jax.nn.softmax(x, axis=axis)

def _gelu(x):
    return jax.nn.gelu(x, approximate=True)

def _silu(x):
    return jax.nn.silu(x)

def _sigmoid(x):
    return jax.nn.sigmoid(x)

def _layernorm(x, axis=-1, eps=1e-05):
    m = jnp.mean(x, axis=axis, keepdims=True)
    v = jnp.var(x, axis=axis, keepdims=True)
    return (x - m) / jnp.sqrt(v + eps)

def _scatter_add(tgt, idx, src, axis=0):
    return tgt.at[idx].add(src)

def _segment_sum(src, seg, n):
    return jax.ops.segment_sum(src, seg, n)
kernel_name = 'mk_decoder_postln_d1_seqx_r4_9bed42'

def setup_inputs(seed: int=0):
    np.random.seed(seed)
    _w = jnp.asarray

    def _rec_inputs():
        import jax
        import jax.numpy as jnp
        _rk = jax.random.key(seed)
        x = -0.000125 + 0.9999 * jax.random.normal(jax.random.fold_in(_rk, 1), (2, 512, 1024), jnp.float32)
        _lenS = 512 - jax.random.randint(jax.random.fold_in(_rk, 7), (2,), 0, max(1, 512 // 4) + 1, jnp.int32)
        _lenS2 = 1024 - jax.random.randint(jax.random.fold_in(_rk, 8), (2,), 0, max(1, 1024 // 4) + 1, jnp.int32)
        _ctx_4096P = jax.random.normal(jax.random.fold_in(_rk, 11), (2, 16, 1024), jnp.float32)
        _ctx_4096c = jax.random.dirichlet(jax.random.fold_in(_rk, 511), 0.3 * jnp.ones((16,), jnp.float32), (2, 1024))
        _ctx_4096t = jnp.einsum('bsk,bkd->bsd', _ctx_4096c, _ctx_4096P)
        _ctx_4096t = _ctx_4096t * jax.lax.rsqrt(jnp.mean(jnp.square(_ctx_4096t)) + 1e-12) * 0.953939
        ctx_4096 = -5.72187e-05 + 0.999849 * (_ctx_4096t + 0.3 * jax.random.normal(jax.random.fold_in(_rk, 611), (2, 1024, 1024), jnp.float32))
        return (x, ctx_4096)
    x, ctx_4096 = _rec_inputs()

    def _L0_attn_setup():
        import jax, jax.numpy as jnp
        import numpy as np
        BLOCK_H = 32
        BLOCK_W = 32
        N_FEAT = 1024
        K_FEAT = 1024
        key = jax.random.key(seed)
        k1, k2, k3 = jax.random.split(key, 3)
        data = jax.random.normal(k1, (4, 256, K_FEAT), dtype=jnp.float32)
        weight = jax.random.normal(k2, (N_FEAT, K_FEAT), dtype=jnp.float32) * 0.02
        nb, kb = (N_FEAT // BLOCK_H, K_FEAT // BLOCK_W)
        block_pattern = jax.random.randint(k3, (nb, kb), 0, 2, dtype=jnp.int32)
        mask = jnp.repeat(jnp.repeat(block_pattern, BLOCK_H, axis=0), BLOCK_W, axis=1)
        return {'data': data, 'weight': weight, 'mask': mask}
    _L0_attn_all = _L0_attn_setup()
    _L0_attn_in = {k: v for k, v in _L0_attn_all.items() if k in ('weight', 'mask')}
    del _L0_attn_all

    def _L0_xattn_setup():
        import jax, jax.numpy as jnp
        import numpy as np
        QMIN = 0.0
        QMAX = 255.0

        def fake_quant(x, scale, zp):
            s = scale.reshape(())
            z = zp.reshape(())
            q = jnp.clip(jnp.round(x / s + z), QMIN, QMAX)
            return (q - z) * s
        key = jax.random.key(seed)
        k1, k2 = jax.random.split(key)
        B, M, K, N = (4, 512, 1024, 1024)
        x1 = jax.random.normal(k1, (B, M, K), dtype=jnp.float32)
        x2 = jax.random.normal(k2, (B, K, N), dtype=jnp.float32)
        x1_scale = jnp.full((1,), 8.0 / 255.0, dtype=jnp.float32)
        x1_zp = jnp.full((1,), 128.0, dtype=jnp.float32)
        x2_scale = jnp.full((1,), 8.0 / 255.0, dtype=jnp.float32)
        x2_zp = jnp.full((1,), 128.0, dtype=jnp.float32)
        return {'x1': x1, 'x2': x2, 'x1_scale': x1_scale, 'x1_zp': x1_zp, 'x2_scale': x2_scale, 'x2_zp': x2_zp}
    _L0_xattn_all = _L0_xattn_setup()
    _L0_xattn_in = {k: v for k, v in _L0_xattn_all.items() if k in ('x1_scale', 'x1_zp', 'x2_scale', 'x2_zp')}
    del _L0_xattn_all

    def _L0_ffn_setup():
        import jax, jax.numpy as jnp
        import numpy as np
        B, S, D_IN, D_OUT = (2, 512, 1024, 1024)
        E, K, R = (8, 2, 16)
        SCALING = 32.0 / 16.0
        key = jax.random.key(seed)
        ks = jax.random.split(key, 6)
        x = jax.random.normal(ks[0], (B, S, D_IN), dtype=jnp.float32)
        gate_w = jax.random.normal(ks[1], (E, D_IN), dtype=jnp.float32) * 0.02
        base_w = jax.random.normal(ks[2], (D_OUT, D_IN), dtype=jnp.float32) * 0.02
        base_b = jax.random.normal(ks[3], (D_OUT,), dtype=jnp.float32) * 0.02
        lora_A = jax.random.normal(ks[4], (E, R, D_IN), dtype=jnp.float32) * 0.02
        lora_B = jax.random.normal(ks[5], (E, D_OUT, R), dtype=jnp.float32) * 0.02
        return {'x': x, 'gate_w': gate_w, 'base_w': base_w, 'base_b': base_b, 'lora_A': lora_A, 'lora_B': lora_B}
    _L0_ffn_all = _L0_ffn_setup()
    _L0_ffn_in = {k: v for k, v in _L0_ffn_all.items() if k in ('gate_w', 'base_w', 'base_b', 'lora_A', 'lora_B')}
    del _L0_ffn_all
    return {'x': x, 'ctx_4096': ctx_4096, 'L0_attn_weight': _L0_attn_in['weight'], 'L0_attn_mask': _L0_attn_in['mask'], 'L0_xattn_x1_scale': _L0_xattn_in['x1_scale'], 'L0_xattn_x1_zp': _L0_xattn_in['x1_zp'], 'L0_xattn_x2_scale': _L0_xattn_in['x2_scale'], 'L0_xattn_x2_zp': _L0_xattn_in['x2_zp'], 'L0_ffn_gate_w': _L0_ffn_in['gate_w'], 'L0_ffn_base_w': _L0_ffn_in['base_w'], 'L0_ffn_base_b': _L0_ffn_in['base_b'], 'L0_ffn_lora_A': _L0_ffn_in['lora_A'], 'L0_ffn_lora_B': _L0_ffn_in['lora_B']}

def reference(x, ctx_4096, L0_attn_weight, L0_attn_mask, L0_xattn_x1_scale, L0_xattn_x1_zp, L0_xattn_x2_scale, L0_xattn_x2_zp, L0_ffn_gate_w, L0_ffn_base_w, L0_ffn_base_b, L0_ffn_lora_A, L0_ffn_lora_B):
    import jax
    import jax.numpy as jnp

    def _L0_attn_ref(data, weight, mask):
        import jax, jax.numpy as jnp
        import numpy as np
        BLOCK_H = 32
        BLOCK_W = 32
        N_FEAT = 1024
        K_FEAT = 1024
        N, K = weight.shape
        nb, kb = (N // BLOCK_H, K // BLOCK_W)
        block_mask = mask.reshape(nb, BLOCK_H, kb, BLOCK_W).astype(jnp.float32).sum(axis=(1, 3)) > 0
        elem_mask = jnp.repeat(jnp.repeat(block_mask, BLOCK_H, axis=0), BLOCK_W, axis=1)
        w_masked = weight * elem_mask.astype(weight.dtype)
        out = jnp.einsum('bsk,nk->bsn', data, w_masked)
        return out

    def _L0_xattn_ref(x1, x2, x1_scale, x1_zp, x2_scale, x2_zp):
        import jax, jax.numpy as jnp
        import numpy as np
        QMIN = 0.0
        QMAX = 255.0

        def fake_quant(x, scale, zp):
            s = scale.reshape(())
            z = zp.reshape(())
            q = jnp.clip(jnp.round(x / s + z), QMIN, QMAX)
            return (q - z) * s
        q1 = fake_quant(x1, x1_scale, x1_zp)
        q2 = fake_quant(x2, x2_scale, x2_zp)
        return jnp.matmul(q1, q2)

    def _L0_ffn_ref(x, gate_w, base_w, base_b, lora_A, lora_B):
        import jax, jax.numpy as jnp
        import numpy as np
        B, S, D_IN, D_OUT = (2, 512, 1024, 1024)
        E, K, R = (8, 2, 16)
        SCALING = 32.0 / 16.0
        gate_logits = jnp.einsum('bsd,ed->bse', x, gate_w)
        weights, selected = jax.lax.top_k(gate_logits, K)
        weights = jax.nn.softmax(weights.astype(jnp.float32), axis=2).astype(x.dtype)
        result = jnp.einsum('bsd,od->bso', x, base_w) + base_b
        w_full = jnp.sum(jax.nn.one_hot(selected, E, dtype=x.dtype) * weights[..., None], axis=2)
        low = jnp.einsum('bsd,erd->ebsr', x, lora_A)
        lora_out = jnp.einsum('ebsr,eor,bse->bso', low, lora_B, w_full)
        result = result + SCALING * lora_out
        return result
    x = _layernorm(x + _L0_attn_ref(x, L0_attn_weight, L0_attn_mask), axis=-1)
    x = _layernorm(x + _L0_xattn_ref(x, ctx_4096, L0_xattn_x1_scale, L0_xattn_x1_zp, L0_xattn_x2_scale, L0_xattn_x2_zp), axis=-1)
    x = _layernorm(x + _L0_ffn_ref(x, L0_ffn_gate_w, L0_ffn_base_w, L0_ffn_base_b, L0_ffn_lora_A, L0_ffn_lora_B), axis=-1)
    return x

_drawn_inputs = setup_inputs


def setup_inputs(seed=0):
    import zlib

    import numpy as np

    out = dict(_drawn_inputs(seed))
    spreads = {}
    factors = {'L0_ffn_base_b': 3.576}
    for name, (base, spread) in spreads.items():
        noise = np.random.default_rng([zlib.crc32(name.encode()), seed]).standard_normal(out[name].shape)
        drawn = base * np.exp(spread * noise) if base else spread * noise
        out[name] = jnp.asarray(drawn.astype(out[name].dtype))
    for name, factor in factors.items():
        out[name] = (out[name] * factor).astype(out[name].dtype)
    return out
```

```python
from contextlib import ExitStack

import concourse.bass as bass
from concourse import mybir

P = 128
D = 1024
TOK = 1024
KC = D // P
TILES = TOK // P
BATCHES = 2
TPB = TILES // BATCHES
HALF = 512
NHALF = D // HALF
BLK = 32
NBLK = D // BLK
EXPERTS, RANK = 8, 16
ER = EXPERTS * RANK
AGW = ER + EXPERTS
SCALING = 32.0 / 16.0
EPS = 1e-5
FIRST = 3
FIRST_ORDER = (1, 0, 2)
RSQRT_MAGIC = float(0x5F3759DF)
CTX_PER_TILE = BATCHES * KC // (TILES - FIRST - 1)

F32 = mybir.dt.float32
F32R = mybir.dt.float32r
BF16 = mybir.dt.bfloat16
F16 = mybir.dt.float16
U8 = mybir.dt.uint8
I32 = mybir.dt.int32
U32 = mybir.dt.uint32
ALU = mybir.AluOpType
ACT = mybir.ActivationFunctionType
AX_X = mybir.AxisListType.X
ds = bass.ds

LN_STEPS = 13
GATE_STEPS = 10


def decoder_layer(nc, xT_first, xT_rest, x_rows, ctx, wT, maskT, qparams, agT, baseT, base_b, lbT, consts, out):
    with ExitStack() as stack:
        def sb(name, cols, dt):
            return stack.enter_context(nc.sbuf_tensor(name, [P, cols], dt))

        def sem(name):
            return stack.enter_context(nc.semaphore(name))

        w_h = sb("w_h", KC * D, F32R)
        w_l = sb("w_l", KC * D, F32R)
        ctx_q = sb("ctx_q", BATCHES * KC * D, BF16)
        resid = sb("resid", TILES * D, F32)
        t_h = sb("t_h", 2 * D, F32R)
        t_l = sb("t_l", 2 * D, F32R)
        t_raw = sb("t_raw", 2 * D, F32)
        w_raw = sb("w_raw", 2 * D, F32)
        c_raw = sb("c_raw", 2 * D, F32)
        corr = sb("corr", D, F32)
        ctx_sum = sb("ctx_sum", BATCHES * D, F16)
        ctx_u8 = sb("ctx_u8", 2 * D, U8)
        q_u8 = sb("q_u8", 2 * D, U8)
        qT = sb("qT", 2 * D, BF16)
        const_sb = sb("const_sb", 2 * P + EXPERTS, F32)
        ident_bf = sb("ident_bf", P, BF16)
        ones_f16 = sb("ones_f16", P, F16)
        par = sb("par", 4, F32)
        par_u8 = sb("par_u8", 4, U8)
        derived = sb("derived", 16, F32)
        mask_rows_sb = sb("mask_rows_sb", 2 * NBLK, F32)
        bn = sb("bn", 12, F32)
        mv = sb("mv", 2, F32)
        scratch = sb("scratch", 8, F32)
        ln1_par = sb("ln1_par", 2 * 8, F32)
        ln2_par = sb("ln2_par", TILES * 2, F32)
        ln3_par = sb("ln3_par", 2, F32)
        low_w = sb("low_w", ER, F32)
        lowT_h = sb("lowT_h", ER, F32R)
        lowT_l = sb("lowT_l", ER, F32R)
        top8 = sb("top8", 8, F32)
        top_i = sb("top_i", 8, U32)
        gate_logits = sb("gate_logits", EXPERTS, F32)
        gate = sb("gate", 8, F32)
        route = sb("route", 3 * EXPERTS, F32)
        with nc.sbuf_tensor("q_rows", [P, TILES * D], BF16) as q_rows:
            pass
        ag_h = sb("ag_h", KC * AGW, F32R)
        ag_l = sb("ag_l", KC * AGW, F32R)
        lb_h = sb("lb_h", D, F32R)
        lb_l = sb("lb_l", D, F32R)

        ps = stack.enter_context(nc.psum_tensor("ps", [P, 8 * HALF], F32))

        def bank(b, cols=HALF, at=0):
            return ps[:, b * HALF + at:b * HALF + at + cols]

        def acc(pair, n):
            return bank(2 * pair + n)

        def acc2(pair):
            return ps[:, pair * D:(pair + 1) * D]

        SUMS = (6, 7)
        COLSUM = 2
        QT_PAIR = (3, 2)
        X2T_PAIR = 2
        LOGITS, LOWT = 6, 7

        ident = const_sb[:, 0:P]
        blockones = const_sb[:, P:2 * P]
        iota = const_sb[:, 2 * P:2 * P + EXPERTS]
        s12, z12 = par[:, 0:2], par[:, 2:4]
        z1, z2 = par[:, 2:3], par[:, 3:4]
        r12, r1, r2 = derived[:, 0:2], derived[:, 0:1], derived[:, 1:2]
        zi12, zi2 = derived[:, 2:4], derived[:, 3:4]
        neg_zi12, neg_zi1 = derived[:, 4:6], derived[:, 4:5]
        zf12, zf1, zf2 = derived[:, 6:8], derived[:, 6:7], derived[:, 7:8]
        ss, col_w, row_w, row_c = (derived[:, i:i + 1] for i in (8, 9, 10, 11))

        consts_loaded = sem("consts_loaded")
        params_loaded = sem("params_loaded")
        mask_loaded = [sem(f"mask_loaded{s}") for s in range(2)]
        w_loaded = [sem(f"w_loaded{s}") for s in range(2)]
        xchunk_loaded = [sem(f"xchunk_loaded{s}") for s in range(2)]
        xT_loaded = [sem(f"xT_loaded{s}") for s in range(2)]
        first_rows_loaded = [sem(f"first_rows_loaded{t}") for t in range(FIRST)]
        rows_loaded = [sem(f"rows_loaded{s}") for s in range(2)]
        ctx_loaded = [sem(f"ctx_loaded{s}") for s in range(2)]
        base_loaded = [sem(f"base_loaded{s}") for s in range(2)]
        ag_loaded = sem("ag_loaded")
        lb_loaded = sem("lb_loaded")
        bias_loaded = sem("bias_loaded")
        out_stored = sem("out_stored")
        par_step = sem("par_step")
        par_ready = sem("par_ready")
        consts_ready = sem("consts_ready")
        c_raw_read = sem("c_raw_read")
        block_sums = sem("block_sums")
        w_masked = sem("w_masked")
        w_hi = sem("w_hi")
        w_lo = sem("w_lo")
        xchunk_hi = sem("xchunk_hi")
        xchunk_lo = sem("xchunk_lo")
        chunk_done = sem("chunk_done")
        xT_hi = sem("xT_hi")
        xT_lo = sem("xT_lo")
        product_done = sem("product_done")
        acc_read = sem("acc_read")
        ln_step = sem("ln_step")
        q_par = sem("q_par")
        q_done = sem("q_done")
        q_rows_done = sem("q_rows_done")
        apply_step = sem("apply_step")
        x1_ready = sem("x1_ready")
        ctx_u8_free = sem("ctx_u8_free")
        ctx_sum_done = sem("ctx_sum_done")
        colsum_done = sem("colsum_done")
        corr_ready = sem("corr_ready")
        resid_added = sem("resid_added")
        q_transposed = sem("q_transposed")
        qT_ready = sem("qT_ready")
        small_hi = sem("small_hi")
        small_lo = sem("small_lo")
        x2_rows = sem("x2_rows")
        x2_transposed = sem("x2_transposed")
        x2T_hi = sem("x2T_hi")
        x2T_lo = sem("x2T_lo")
        logits_done = sem("logits_done")
        gate_step = sem("gate_step")
        gate_diff = sem("gate_diff")
        gate_exp = sem("gate_exp")
        low_ready = sem("low_ready")
        low_transposed = sem("low_transposed")
        lowT_hi = sem("lowT_hi")
        lowT_lo = sem("lowT_lo")
        half_done = sem("half_done")
        x3_ready = sem("x3_ready")

        def cols(tensor, i, width=D):
            return tensor[:, ds(i * width, width)]

        def xchunk_cols(slot):
            return slice(slot * FIRST * P, (slot + 1) * FIRST * P)

        block = stack.enter_context(nc.Block())

        @block.sync
        def _(sp):
            sp.dma_start(par[:], qparams.partition_broadcast(P)).then_inc(params_loaded, 16)
            sp.dma_start(const_sb[:], consts).then_inc(consts_loaded, 16)

            def load_chunk(k, s, reuse):
                if reuse:
                    sp.wait_ge(c_raw_read, k - 1)
                sp.dma_start(cols(c_raw, s).bitcast(I32), maskT[ds(k * P, P), :]).then_inc(mask_loaded[s], 16)
                if reuse:
                    sp.wait_ge(w_lo, k - 1)
                sp.dma_start(cols(w_raw, s), wT[ds(k * P, P), :]).then_inc(w_loaded[s], 16)
                if reuse:
                    sp.wait_ge(xchunk_lo, k - 1)
                sp.dma_start(t_raw[:, xchunk_cols(s)], xT_first[ds(k * P, P), :]).then_inc(xchunk_loaded[s], 16)

            load_chunk(0, 0, False)
            load_chunk(1, 1, False)
            with sp.Fori(1, KC // 2) as j:
                for s in range(2):
                    load_chunk(2 * j + s, s, True)

            sp.dma_start(cols(t_raw, 1), xT_rest[0:P, :]).then_inc(xT_loaded[1], 16)
            for t in FIRST_ORDER:
                sp.dma_start(cols(resid, t), x_rows[t * P:(t + 1) * P, :]).then_inc(first_rows_loaded[t], 16)

            sp.wait_ge(xchunk_lo, KC)
            sp.wait_ge(c_raw_read, KC)
            with sp.Fori(2, TILES // 2) as j:
                for s in range(2):
                    t = 2 * j + s
                    sp.wait_ge(xT_lo, t - FIRST)
                    sp.dma_start(cols(t_raw, s), xT_rest[ds((t - FIRST) * P, P), :]).then_inc(xT_loaded[s], 16)
                    sp.wait_ge(acc_read, t - 2)
                    sp.dma_start(cols(resid, t - 1), x_rows[ds((t - 1) * P, P), :]).then_inc(rows_loaded[1 - s], 16)
                    for i in range(CTX_PER_TILE):
                        c = CTX_PER_TILE * (t - 4) + i
                        sp.wait_ge(c_raw_read, KC + c - 1)
                        sp.dma_start(cols(c_raw, i % 2), ctx[ds(c * P, P), :]).then_inc(ctx_loaded[i % 2], 16)
            sp.wait_ge(acc_read, TILES - 2)
            sp.dma_start(cols(resid, TILES - 1), x_rows[(TILES - 1) * P:, :]).then_inc(rows_loaded[1], 16)

            with sp.Fori(0, KC // 2) as j:
                for s in range(2):
                    k = 2 * j + s
                    sp.wait_ge(w_lo, KC + k - 1)
                    sp.dma_start(cols(w_raw, s), baseT[ds(k * P, P), :]).then_inc(base_loaded[s], 16)
            sp.wait_ge(c_raw_read, KC + BATCHES * KC)
            sp.dma_start(c_raw[:, 0:KC * AGW], agT).then_inc(ag_loaded, 16)
            sp.wait_ge(w_lo, 2 * KC - 1)
            sp.dma_start(cols(w_raw, 0), lbT).then_inc(lb_loaded, 16)
            sp.wait_ge(resid_added, TILES)
            sp.dma_start(corr[:], base_b.partition_broadcast(P)).then_inc(bias_loaded, 16)

            with sp.Fori(0, TILES) as t:
                sp.wait_ge(x3_ready, t + 1)
                sp.dma_start(out[ds(t * P, P), :], cols(resid, t)).then_inc(out_stored, 16)
            sp.wait_ge(out_stored, 16 * TILES)

        @block.vector
        def _(dve):
            def rsqrt_newton(first_step, v, nv, rstd_out):
                r = scratch[:, 2:3]
                dve.wait_ge(ln_step, first_step)
                dve.tensor_scalar(r.bitcast(I32), v.bitcast(I32), -0.5, RSQRT_MAGIC, ALU.mult, ALU.add).then_inc(ln_step, 1)
                for n in range(3):
                    new = rstd_out if n == 2 else scratch[:, 4 + n:5 + n]
                    dve.wait_ge(ln_step, first_step + 1 + 2 * n)
                    dve.scalar_tensor_tensor(scratch[:, 3:4], r, nv, r, ALU.mult, ALU.mult).then_inc(ln_step, 1)
                    dve.wait_ge(ln_step, first_step + 2 + 2 * n)
                    dve.scalar_tensor_tensor(new, scratch[:, 3:4], 1.5, r, ALU.add, ALU.mult).then_inc(ln_step, 1)
                    r = new

            def row_half_stats(n, row):
                dve.bn_stats(bn[:, 6 * n:6 * n + 6], row).then_inc(ln_step, 1)

            def row_stats(index, rstd_out, nmr_out):
                base = index * LN_STEPS
                dve.drain()
                dve.bn_aggr(mv[:], bn[:]).then_inc(ln_step, 1)
                dve.wait_ge(ln_step, base + 3)
                v, nv = scratch[:, 0:1], scratch[:, 1:2]
                dve.tensor_scalar(v, mv[:, 1:2], EPS, None, ALU.add).then_inc(ln_step, 1)
                dve.tensor_scalar(nv, mv[:, 1:2], EPS, -0.5, ALU.add, ALU.mult).then_inc(ln_step, 1)
                rsqrt_newton(base + 5, v, nv, rstd_out)
                dve.wait_ge(ln_step, base + 12)
                dve.scalar_tensor_tensor(nmr_out, mv[:, 0:1], -1.0, rstd_out, ALU.mult, ALU.mult).then_inc(ln_step, 1)

            dve.wait_ge(params_loaded, 16)
            dve.reciprocal(r12, s12).then_inc(par_step, 1)
            dve.tensor_copy(par_u8[:, 0:2], z12).then_inc(par_step, 1)
            dve.tensor_tensor(ss, par[:, 0:1], par[:, 1:2], ALU.mult).then_inc(par_step, 1)
            dve.wait_ge(par_step, 3)
            dve.tensor_copy(zi12, par_u8[:, 0:2]).then_inc(par_step, 1)
            dve.wait_ge(par_step, 4)
            dve.tensor_scalar(neg_zi12, zi12, -1.0, None, ALU.mult).then_inc(par_step, 1)
            dve.tensor_tensor(zf12, z12, zi12, ALU.subtract).then_inc(par_step, 1)
            dve.wait_ge(par_step, 6)
            dve.scalar_tensor_tensor(col_w, zf1, -1.0, ss, ALU.mult, ALU.mult).then_inc(par_step, 1)
            dve.scalar_tensor_tensor(row_w, zf2, -1.0, ss, ALU.mult, ALU.mult).then_inc(par_step, 1)
            dve.wait_ge(par_step, 8)
            dve.scalar_tensor_tensor(row_c, row_w, -float(D), zf1, ALU.mult, ALU.mult).then_inc(par_step, 1)
            dve.wait_ge(par_step, 9)
            dve.memset(ctx_u8[:, 0:1], 0.0).then_inc(ctx_u8_free, 2)
            dve.memset(ones_f16[:], 1.0).then_inc(par_ready, 1)
            dve.wait_ge(consts_loaded, 16)
            dve.tensor_copy(ident_bf[:], ident).then_inc(consts_ready, 1)

            def sum_mask_rows(s, loads):
                dve.wait_ge(mask_loaded[s], 16 * loads)
                dve.tensor_reduce(cols(mask_rows_sb, s, NBLK),
                                  cols(c_raw, s).bitcast(I32).rearrange("p (b c) -> p b c", c=BLK),
                                  AX_X, ALU.add).then_inc(c_raw_read, 1)

            def mask_chunk(k, s, loads, more=True):
                dve.wait_ge(block_sums, k + 1)
                dve.wait_ge(w_loaded[s], 16 * loads)
                w = cols(w_raw, s).rearrange("p (b c) -> p b c", c=BLK)
                sums = bank(SUMS[s], NBLK).unsqueeze(2).to_broadcast([P, NBLK, BLK])
                dve.scalar_tensor_tensor(w, sums, 0.0, w, ALU.is_gt, ALU.mult).then_inc(w_masked, 1)
                if more:
                    sum_mask_rows(1 - s, loads + s)
                dve.wait_ge(w_hi, k + 1)
                dve.tensor_tensor(cols(w_l, k), cols(w_raw, s), cols(w_h, k).bitcast(F32),
                                  ALU.subtract).then_inc(w_lo, 1)

            sum_mask_rows(0, 1)
            with dve.Fori(0, KC // 2 - 1) as j:
                for s in range(2):
                    mask_chunk(2 * j + s, s, j + 1)
            mask_chunk(KC - 2, 0, KC // 2)
            mask_chunk(KC - 1, 1, KC // 2, more=False)

            def ln1(o, t, s, pair):
                par1 = ln1_par[:, 8 * s:8 * s + 8]
                dve.wait_ge(product_done, o + 1)
                dve.tensor_tensor(cols(resid, t), acc2(pair), cols(resid, t), ALU.add).then_inc(acc_read, 1)
                dve.drain()
                for n in range(NHALF):
                    row_half_stats(n, resid[:, ds(t * D + n * HALF, HALF)])
                row_stats(o, par1[:, 0:1], par1[:, 1:2])
                dve.wait_ge(ln_step, (o + 1) * LN_STEPS)
                dve.tensor_tensor(par1[:, 2:3], par1[:, 0:1], r1, ALU.mult).then_inc(q_par, 1)
                dve.tensor_scalar(par1[:, 3:4], par1[:, 1:2], r1, z1, ALU.mult, ALU.add).then_inc(q_par, 1)

            def apply1(o, t, s):
                par1 = ln1_par[:, 8 * s:8 * s + 8]
                dve.wait_ge(q_rows_done, o + 1)
                dve.tensor_scalar(par1[:, 5:6], par1[:, 4:5], row_w, row_c, ALU.mult, ALU.add).then_inc(apply_step, 1)
                dve.wait_ge(apply_step, 2 * o + 1)
                dve.tensor_tensor(par1[:, 6:7], par1[:, 5:6], par1[:, 1:2], ALU.add).then_inc(apply_step, 1)
                dve.wait_ge(apply_step, 2 * o + 2)
                dve.tensor_scalar(cols(resid, t), cols(resid, t), par1[:, 0:1], par1[:, 6:7],
                                  ALU.mult, ALU.add).then_inc(x1_ready, 1)

            for o in range(FIRST):
                dve.wait_ge(first_rows_loaded[FIRST_ORDER[o]], 16)
                ln1(o, FIRST_ORDER[o], o % 2, FIRST_ORDER[o])
                if o:
                    apply1(o - 1, FIRST_ORDER[o - 1], (o - 1) % 2)
            with dve.Fori(2, TILES // 2) as j:
                for s in range(2):
                    t = 2 * j + s
                    for i in range(CTX_PER_TILE):
                        c = CTX_PER_TILE * (t - 4) + i
                        dve.wait_ge(c_raw_read, KC + c + 1)
                        dve.tensor_scalar(cols(ctx_q, c), cols(ctx_u8, i % 2), zi2, None,
                                          ALU.subtract).then_inc(ctx_u8_free, 1)
                    dve.wait_ge(rows_loaded[1 - s], 16 * (j - 1))
                    ln1(t - 1, t - 1, 1 - s, 1 - s)
                    apply1(t - 2, t - 2, s)
            dve.wait_ge(rows_loaded[1], 16 * (TILES // 2 - 1))
            ln1(TILES - 1, TILES - 1, 1, 1)
            apply1(TILES - 2, TILES - 2, 0)
            apply1(TILES - 1, TILES - 1, 1)

            with dve.Fori(0, TILES // 2) as j:
                for s in range(2):
                    t = 2 * j + s
                    dve.wait_ge(resid_added, t + 1)
                    dve.wait_ge(product_done, TILES + t + 1)
                    dve.scalar_tensor_tensor(cols(resid, t), acc2(s), ss, cols(resid, t),
                                             ALU.mult, ALU.add).then_inc(acc_read, 1)
                    dve.drain()
                    for n in range(NHALF):
                        row_half_stats(n, resid[:, ds(t * D + n * HALF, HALF)])
                    row_stats(TILES + t, cols(ln2_par, 2 * t, 1), cols(ln2_par, 2 * t + 1, 1))

            def split_x2T(t, s):
                for n in range(NHALF):
                    dve.wait_ge(x2T_hi, NHALF * t + n + 1)
                    dve.tensor_tensor(t_l[:, s * D + n * HALF:s * D + (n + 1) * HALF], acc(X2T_PAIR, n),
                                      t_h[:, s * D + n * HALF:s * D + (n + 1) * HALF].bitcast(F32),
                                      ALU.subtract).then_inc(x2T_lo, 1)

            def route_tokens(t):
                base = t * GATE_STEPS
                dve.wait_ge(logits_done, t + 1)
                dve.tensor_copy(gate_logits[:], bank(LOGITS, EXPERTS, at=ER)).then_inc(gate_step, 1)
                dve.drain()
                dve.max(top8[:], gate_logits[:]).then_inc(gate_step, 1)
                dve.wait_ge(gate_step, base + 2)
                dve.tensor_tensor(gate[:, 0:1], top8[:, 1:2], top8[:, 0:1], ALU.subtract).then_inc(gate_diff, 1)
                dve.max_index(top_i[:], top8[:], gate_logits[:]).then_inc(gate_step, 1)
                dve.wait_ge(gate_step, base + 3)
                dve.tensor_copy(gate[:, 2:4], top_i[:, 0:2]).then_inc(gate_step, 1)
                dve.wait_ge(gate_exp, t + 1)
                dve.tensor_scalar(gate[:, 4:5], gate[:, 1:2], 1.0, None, ALU.add).then_inc(gate_step, 1)
                dve.wait_ge(gate_step, base + 5)
                dve.reciprocal(gate[:, 5:6], gate[:, 4:5]).then_inc(gate_step, 1)
                dve.wait_ge(gate_step, base + 6)
                dve.tensor_tensor(gate[:, 6:7], gate[:, 1:2], gate[:, 5:6], ALU.mult).then_inc(gate_step, 1)
                dve.tensor_scalar(route[:, 0:EXPERTS], iota, gate[:, 2:3], gate[:, 5:6],
                                  ALU.is_equal, ALU.mult).then_inc(gate_step, 1)
                dve.wait_ge(gate_step, base + 7)
                dve.tensor_scalar(route[:, EXPERTS:2 * EXPERTS], iota, gate[:, 3:4], gate[:, 6:7],
                                  ALU.is_equal, ALU.mult).then_inc(gate_step, 1)
                dve.wait_ge(gate_step, base + 9)
                dve.tensor_tensor(route[:, 2 * EXPERTS:], route[:, 0:EXPERTS], route[:, EXPERTS:2 * EXPERTS],
                                  ALU.add).then_inc(gate_step, 1)
                dve.wait_ge(gate_step, base + 10)
                dve.scalar_tensor_tensor(low_w[:].rearrange("p (e r) -> p e r", r=RANK),
                                         bank(LOGITS, ER).rearrange("p (e r) -> p e r", r=RANK), SCALING,
                                         route[:, 2 * EXPERTS:].unsqueeze(2).to_broadcast([P, EXPERTS, RANK]),
                                         ALU.mult, ALU.mult).then_inc(low_ready, 1)

            def mixture_rows(t, s, more=True):
                route_tokens(t)
                dve.wait_ge(lowT_hi, t + 1)
                dve.tensor_tensor(lowT_l[:], bank(LOWT, P), lowT_h[:].bitcast(F32), ALU.subtract).then_inc(lowT_lo, 1)
                if more:
                    split_x2T(t + 1, 1 - s)
                halves = [resid[:, ds(t * D + n * HALF, HALF)] for n in range(NHALF)]
                dve.wait_ge(resid_added, TILES + t + 1)
                dve.wait_ge(half_done, t + 1)
                dve.tensor_tensor(halves[0], acc(s, 0), halves[0], ALU.add)
                dve.drain()
                row_half_stats(0, halves[0])
                dve.wait_ge(product_done, 2 * TILES + t + 1)
                dve.tensor_tensor(halves[1], acc(s, 1), halves[1], ALU.add).then_inc(acc_read, 1)
                dve.drain()
                row_half_stats(1, halves[1])
                row_stats(2 * TILES + t, ln3_par[:, 0:1], ln3_par[:, 1:2])
                dve.wait_ge(ln_step, (2 * TILES + t + 1) * LN_STEPS)
                dve.tensor_scalar(cols(resid, t), cols(resid, t), ln3_par[:, 0:1], ln3_par[:, 1:2],
                                  ALU.mult, ALU.add).then_inc(x3_ready, 1)

            split_x2T(0, 0)
            with dve.Fori(0, TILES // 2 - 1) as j:
                for s in range(2):
                    mixture_rows(2 * j + s, s)
            mixture_rows(TILES - 2, 0)
            mixture_rows(TILES - 1, 1, more=False)

        @block.scalar
        def _(act):
            def round_chunk(k, s, loads, reuse):
                act.wait_ge(xchunk_loaded[s], 16 * loads)
                if reuse:
                    act.wait_ge(chunk_done, k - 1)
                nc.scalar.activation(t_h[:, xchunk_cols(s)], t_raw[:, xchunk_cols(s)], ACT.Copy).then_inc(xchunk_hi, 1)
                act.wait_ge(w_masked, k + 1)
                nc.scalar.activation(cols(w_h, k), cols(w_raw, s), ACT.Copy).then_inc(w_hi, 1)

            round_chunk(0, 0, 1, False)
            round_chunk(1, 1, 1, False)
            with act.Fori(1, KC // 2) as j:
                for s in range(2):
                    round_chunk(2 * j + s, s, j + 1, True)

            act.wait_ge(xT_loaded[1], 16)
            nc.scalar.activation(cols(t_h, 1), cols(t_raw, 1), ACT.Copy).then_inc(xT_hi, 1)

            def quantise_rows(o, t, s):
                par1 = ln1_par[:, 8 * s:8 * s + 8]
                act.wait_ge(q_par, 2 * o + 2)
                nc.scalar.activation(cols(q_u8, s), cols(resid, t), ACT.Identity, bias=par1[:, 3:4],
                                     scale=par1[:, 2:3]).then_inc(q_done, 1)
                act.wait_ge(q_done, o + 1)
                nc.scalar.activation(cols(q_rows, t), cols(q_u8, s), ACT.Identity, bias=neg_zi1,
                                     accum_out=par1[:, 4:5]).then_inc(q_rows_done, 1)

            quantise_rows(0, FIRST_ORDER[0], 0)
            quantise_rows(1, FIRST_ORDER[1], 1)
            with act.Fori(2, TILES // 2) as j:
                for s in range(2):
                    t = 2 * j + s
                    act.wait_ge(xT_loaded[s], 16 * (j - 1 + s))
                    act.wait_ge(product_done, t - 1)
                    nc.scalar.activation(cols(t_h, s), cols(t_raw, s), ACT.Copy).then_inc(xT_hi, 1)
                    for i in range(CTX_PER_TILE):
                        c = CTX_PER_TILE * (t - 4) + i
                        act.wait_ge(ctx_loaded[i % 2], 16 * (CTX_PER_TILE // 2 * (t - 4) + i // 2 + 1))
                        act.wait_ge(par_ready, 1)
                        act.wait_ge(ctx_u8_free, c + 1)
                        nc.scalar.activation(cols(ctx_u8, i % 2), cols(c_raw, i % 2), ACT.Identity, bias=z2,
                                             scale=r2).then_inc(c_raw_read, 1)
                    quantise_rows(t - 2, t - 2, s)
            quantise_rows(TILES - 2, TILES - 2, 0)

            def column_correction(b):
                act.wait_ge(colsum_done, b + 1)
                if b:
                    act.wait_ge(resid_added, b * TPB)
                nc.scalar.activation(corr[:], acc2(COLSUM), ACT.Copy, scale=col_w).then_inc(corr_ready, 1)

            def stage2_tile(t, s, loads):
                act.wait_ge(q_transposed, t + 1)
                act.wait_ge(product_done, TILES + t - 1)
                nc.scalar.activation(cols(qT, s), acc2(QT_PAIR[s]), ACT.Copy).then_inc(qT_ready, 1)
                act.wait_ge(base_loaded[s], 16 * loads)
                nc.scalar.activation(cols(w_h, t), cols(w_raw, s), ACT.Copy).then_inc(w_hi, 1)

            column_correction(0)
            quantise_rows(TILES - 1, TILES - 1, 1)
            with act.Fori(0, TPB // 2) as j:
                for s in range(2):
                    stage2_tile(2 * j + s, s, j + 1)
            column_correction(1)
            with act.Fori(TPB // 2, TILES // 2) as j:
                for s in range(2):
                    stage2_tile(2 * j + s, s, j + 1)

            act.wait_ge(q_transposed, TILES)
            act.wait_ge(ag_loaded, 16)
            nc.scalar.activation(ag_h[:], c_raw[:, 0:KC * AGW], ACT.Copy).then_inc(small_hi, 1)

            def normalise2(t, s):
                act.wait_ge(ln_step, (TILES + t + 1) * LN_STEPS)
                act.wait_ge(resid_added, TILES + t - 1)
                nc.scalar.activation(cols(t_raw, s), cols(resid, t), ACT.Identity, bias=cols(ln2_par, 2 * t + 1, 1),
                                     scale=cols(ln2_par, 2 * t, 1)).then_inc(x2_rows, 1)

            def round_x2T(t, s):
                act.wait_ge(product_done, 2 * TILES + t - 1)
                for n in range(NHALF):
                    act.wait_ge(x2_transposed, NHALF * t + n + 1)
                    nc.scalar.activation(t_h[:, s * D + n * HALF:s * D + (n + 1) * HALF], acc(X2T_PAIR, n),
                                         ACT.Copy).then_inc(x2T_hi, 1)

            def mixture_tile(t, s, more=True):
                if more:
                    normalise2(t + 1, 1 - s)
                act.wait_ge(gate_diff, t + 1)
                nc.scalar.activation(gate[:, 1:2], gate[:, 0:1], ACT.Exp).then_inc(gate_exp, 1)
                act.wait_ge(low_transposed, t + 1)
                nc.scalar.activation(lowT_h[:], bank(LOWT, P), ACT.Copy).then_inc(lowT_hi, 1)
                if more:
                    round_x2T(t + 1, 1 - s)

            normalise2(0, 0)
            round_x2T(0, 0)
            act.wait_ge(lb_loaded, 16)
            nc.scalar.activation(lb_h[:], cols(w_raw, 0), ACT.Copy).then_inc(small_hi, 1)
            with act.Fori(0, TILES // 2 - 1) as j:
                for s in range(2):
                    mixture_tile(2 * j + s, s)
            mixture_tile(TILES - 2, 0)
            mixture_tile(TILES - 1, 1, more=False)

        @block.gpsimd
        def _(pool):
            def low_part(out, raw, high):
                return pool.tensor_tensor(out, raw, high.bitcast(F32), ALU.subtract)

            def split_xchunk(k, s):
                pool.wait_ge(xchunk_hi, k + 1)
                low_part(t_l[:, xchunk_cols(s)], t_raw[:, xchunk_cols(s)], t_h[:, xchunk_cols(s)]).then_inc(xchunk_lo, 1)

            with pool.Fori(0, KC // 2) as j:
                for s in range(2):
                    split_xchunk(2 * j + s, s)
            pool.wait_ge(xT_hi, 1)
            low_part(cols(t_l, 1), cols(t_raw, 1), cols(t_h, 1)).then_inc(xT_lo, 1)

            with pool.Fori(2, TILES // 2) as j:
                for s in range(2):
                    t = 2 * j + s
                    pool.wait_ge(xT_hi, t - FIRST + 1)
                    low_part(cols(t_l, s), cols(t_raw, s), cols(t_h, s)).then_inc(xT_lo, 1)
                    total = cols(ctx_sum, j - 2)
                    for i in range(CTX_PER_TILE):
                        nth = CTX_PER_TILE * s + i
                        if nth == 0:
                            continue
                        c = KC * (j - 2) + nth
                        pool.wait_ge(ctx_u8_free, 2 + c + 1)
                        if nth > 1:
                            pool.wait_ge(ctx_sum_done, (KC - 1) * (j - 2) + nth - 1)
                        pool.tensor_tensor(total, cols(ctx_q, KC * (j - 2)) if nth == 1 else total,
                                           cols(ctx_q, c), ALU.add).then_inc(ctx_sum_done, 1)

            pool.wait_ge(x1_ready, len(FIRST_ORDER))
            for b in range(BATCHES):
                pool.wait_ge(corr_ready, b + 1)
                with pool.Fori(b * TPB // 2, (b + 1) * TPB // 2) as j:
                    for s in range(2):
                        t = 2 * j + s
                        pool.wait_ge(x1_ready, t + 1)
                        pool.tensor_tensor(cols(resid, t), cols(resid, t), corr[:], ALU.add).then_inc(resid_added, 1)
                        pool.wait_ge(w_hi, KC + t + 1)
                        low_part(cols(w_l, t), cols(w_raw, s), cols(w_h, t)).then_inc(w_lo, 1)
            pool.wait_ge(small_hi, 1)
            low_part(ag_l[:], c_raw[:, 0:KC * AGW], ag_h[:]).then_inc(small_lo, 1)
            pool.wait_ge(small_hi, 2)
            low_part(lb_l[:], cols(w_raw, 0), lb_h[:]).then_inc(small_lo, 1)

            pool.wait_ge(bias_loaded, 16)
            with pool.Fori(0, TILES // 2) as j:
                for s in range(2):
                    t = 2 * j + s
                    pool.wait_ge(x2_rows, t + 1)
                    pool.tensor_tensor(cols(resid, t), cols(t_raw, s), corr[:], ALU.add).then_inc(resid_added, 1)

        @block.tensor
        def _(pe):
            def w_half(tensor, k, n):
                return tensor[:, ds(k * D + n * HALF, HALF)]

            def sum_mask_blocks(k, s):
                pe.wait_ge(c_raw_read, k + 1)
                pe.matmul(bank(SUMS[s], NBLK), blockones, cols(mask_rows_sb, s, NBLK),
                          start=True, stop=True).then_inc(block_sums, 1)

            def chunk_cols(s, t):
                return slice((s * FIRST + t) * P, (s * FIRST + t + 1) * P)

            def chunk_products(k, s, start=False, stop=False):
                pe.wait_ge(w_hi, k + 1)
                for t in FIRST_ORDER:
                    for n in range(NHALF):
                        pe.matmul(acc(t, n), t_h[:, chunk_cols(s, t)], w_half(w_h, k, n), start=start, stop=False)
                if not stop:
                    sum_mask_blocks(k + 1, 1 - s)
                pe.wait_ge(xchunk_lo, k + 1)
                pe.wait_ge(w_lo, k + 1)
                for t in FIRST_ORDER:
                    for n in range(NHALF):
                        pe.matmul(acc(t, n), t_l[:, chunk_cols(s, t)], w_half(w_h, k, n), start=False, stop=False)
                        last = pe.matmul(acc(t, n), t_h[:, chunk_cols(s, t)], w_half(w_l, k, n),
                                         start=False, stop=stop)
                    if stop:
                        last.then_inc(product_done, 1)
                if not stop:
                    last.then_inc(chunk_done, 1)

            pe.wait_ge(consts_loaded, 16)
            sum_mask_blocks(0, 0)
            chunk_products(0, 0, start=True)
            chunk_products(1, 1)
            with pe.Fori(1, KC // 2 - 1) as j:
                for s in range(2):
                    chunk_products(2 * j + s, s)
            chunk_products(KC - 2, 0)
            chunk_products(KC - 1, 1, stop=True)

            def split_product(s, n, chunks, stop):
                for k in chunks:
                    hi = t_h[:, s * D + k * P:s * D + (k + 1) * P]
                    lo = t_l[:, s * D + k * P:s * D + (k + 1) * P]
                    pe.matmul(acc(s, n), hi, w_half(w_h, k, n), start=(k == 0), stop=False)
                    pe.matmul(acc(s, n), hi, w_half(w_l, k, n), start=False, stop=False)
                    last = pe.matmul(acc(s, n), lo, w_half(w_h, k, n), start=False, stop=(stop and k == KC - 1))
                return last

            def stage1_tile(t, s, reads):
                pe.wait_ge(acc_read, reads)
                pe.wait_ge(xT_hi, t - FIRST + 1)
                pe.wait_ge(xT_lo, t - FIRST + 1)
                for n in range(NHALF):
                    last = split_product(s, n, range(KC), True)
                last.then_inc(product_done, 1)

            stage1_tile(FIRST, 1, 1)
            with pe.Fori(2, TILES // 2) as j:
                for s in range(2):
                    stage1_tile(2 * j + s, s, 2 * j + s - 1)

            def column_sums(b):
                pe.wait_ge(ctx_sum_done, (KC - 1) * (b + 1))
                for n in range(NHALF):
                    last = pe.matmul(acc(COLSUM, n), ones_f16[:], ctx_sum[:, b * D + n * HALF:b * D + (n + 1) * HALF],
                                     start=True, stop=True)
                last.then_inc(colsum_done, 1)

            def transpose_q(t, s):
                pe.wait_ge(q_rows_done, t + 1)
                for k in range(KC):
                    last = pe.matmul(ps[:, QT_PAIR[s] * D + k * P:QT_PAIR[s] * D + (k + 1) * P],
                                     q_rows[:, ds(t * D + k * P, P)], ident_bf[:], start=True, stop=True,
                                     skip_group_check=True)
                last.then_inc(q_transposed, 1)

            def stage2_product(t, s, b):
                pe.wait_ge(qT_ready, t + 1)
                pe.wait_ge(acc_read, TILES + t - 1)
                for n in range(NHALF):
                    for k in range(KC):
                        last = pe.matmul(acc(s, n), qT[:, s * D + k * P:s * D + (k + 1) * P],
                                         w_half(ctx_q, b * KC + k, n), start=(k == 0), stop=(k == KC - 1))
                last.then_inc(product_done, 1)

            pe.wait_ge(par_ready, 1)
            pe.wait_ge(consts_ready, 1)
            column_sums(0)
            pe.wait_ge(q_rows_done, FIRST)
            transpose_q(0, 0)
            pe.wait_ge(corr_ready, 1)
            with pe.Fori(0, TPB // 2) as j:
                transpose_q(2 * j + 1, 1)
                stage2_product(2 * j, 0, 0)
                transpose_q(2 * j + 2, 0)
                stage2_product(2 * j + 1, 1, 0)
            column_sums(1)
            pe.wait_ge(corr_ready, 2)
            for t in range(TPB, TILES, 2):
                transpose_q(t + 1, 1)
                stage2_product(t, 0, 1)
                if t + 2 < TILES:
                    transpose_q(t + 2, 0)
                stage2_product(t + 1, 1, 1)

            def transpose_x2(t, s):
                pe.wait_ge(x2_rows, t + 1)
                for n in range(NHALF):
                    for k in range(n * KC // 2, (n + 1) * KC // 2):
                        last = pe.transpose(ps[:, X2T_PAIR * D + k * P:X2T_PAIR * D + (k + 1) * P],
                                            t_raw[:, s * D + k * P:s * D + (k + 1) * P], ident)
                    last.then_inc(x2_transposed, 1)

            def low_and_logits(t, s):
                pe.wait_ge(x2T_hi, NHALF * (t + 1))
                pe.wait_ge(x2T_lo, NHALF * (t + 1))
                for k in range(KC):
                    hi = t_h[:, s * D + k * P:s * D + (k + 1) * P]
                    lo = t_l[:, s * D + k * P:s * D + (k + 1) * P]
                    high, low = (a[:, k * AGW:(k + 1) * AGW] for a in (ag_h, ag_l))
                    pe.matmul(bank(LOGITS, AGW), hi, high, start=(k == 0), stop=False)
                    pe.matmul(bank(LOGITS, AGW), hi, low, start=False, stop=False)
                    last = pe.matmul(bank(LOGITS, AGW), lo, high, start=False, stop=(k == KC - 1))
                last.then_inc(logits_done, 1)

            def lora_product(s, n):
                half = slice(n * HALF, (n + 1) * HALF)
                pe.matmul(acc(s, n), lowT_h[:], lb_h[:, half], start=False, stop=False)
                pe.matmul(acc(s, n), lowT_h[:], lb_l[:, half], start=False, stop=False)
                return pe.matmul(acc(s, n), lowT_l[:], lb_h[:, half], start=False, stop=True)

            def stage3_tile(t, s, more=True):
                low_and_logits(t, s)
                pe.wait_ge(acc_read, 2 * TILES + t - 1)
                split_product(s, 0, range(KC), False)
                pe.wait_ge(low_ready, t + 1)
                pe.transpose(bank(LOWT, P), low_w[:], ident).then_inc(low_transposed, 1)
                if more:
                    transpose_x2(t + 1, 1 - s)
                split_product(s, 1, range(KC // 2), False)
                pe.wait_ge(lowT_hi, t + 1)
                pe.wait_ge(lowT_lo, t + 1)
                pe.wait_ge(small_lo, 2)
                lora_product(s, 0).then_inc(half_done, 1)
                split_product(s, 1, range(KC // 2, KC), False)
                lora_product(s, 1).then_inc(product_done, 1)

            transpose_x2(0, 0)
            pe.wait_ge(small_lo, 1)
            pe.wait_ge(w_lo, 2 * KC)
            with pe.Fori(0, TILES // 2 - 1) as j:
                for s in range(2):
                    stage3_tile(2 * j + s, s)
            stage3_tile(TILES - 2, 0)
            stage3_tile(TILES - 1, 1, more=False)


def kernel(**inputs):
    import numpy as np
    import concourse.bacc as bacc
    from concourse.bass_utils import run_bass_kernel_spmd

    def arr(name):
        return np.asarray(inputs[name])

    x_rows = arr("x").reshape(TOK, D)
    rows = np.arange(P)
    consts = np.concatenate([np.eye(P), (rows[:, None] // BLK == rows[None, :] // BLK),
                             np.broadcast_to(np.arange(EXPERTS), (P, EXPERTS))], axis=1).astype(np.float32)
    laid_out = {
        "xT_first": x_rows[:FIRST * P].T,
        "xT_rest": x_rows[FIRST * P:].reshape(TILES - FIRST, P, KC, P).transpose(0, 3, 2, 1).reshape(-1, D),
        "x_rows": x_rows,
        "ctx": arr("ctx_4096").reshape(BATCHES * D, D),
        "wT": arr("L0_attn_weight").T,
        "maskT": arr("L0_attn_mask").T,
        "qparams": np.concatenate([arr("L0_xattn_x1_scale"), arr("L0_xattn_x2_scale"),
                                   arr("L0_xattn_x1_zp"), arr("L0_xattn_x2_zp")]),
        "agT": np.concatenate([arr("L0_ffn_lora_A").reshape(ER, D), arr("L0_ffn_gate_w")], axis=0)
                 .T.reshape(KC, P, AGW).transpose(1, 0, 2).reshape(P, KC * AGW),
        "baseT": arr("L0_ffn_base_w").T,
        "base_b": arr("L0_ffn_base_b"),
        "lbT": arr("L0_ffn_lora_B").transpose(0, 2, 1).reshape(ER, D),
        "consts": consts,
    }
    nc = bacc.Bacc("TRN2", target_bir_lowering=False, num_devices=1)
    arrays, args = {}, []
    for name, a in laid_out.items():
        a = np.ascontiguousarray(a)
        arrays[f"in_{name}"] = a
        args.append(nc.dram_tensor(f"in_{name}", a.shape, mybir.dt.from_np(a.dtype), kind="ExternalInput").ap())
    out = nc.dram_tensor("out", (TOK, D), F32, kind="ExternalOutput").ap()
    decoder_layer(nc, *args, out)
    result = run_bass_kernel_spmd(nc, [arrays], core_ids=[0])
    return result.results[0]["out"].reshape(BATCHES, TOK // BATCHES, D)
```

```python
from contextlib import ExitStack

import concourse.bass as bass
from concourse import mybir

P = 128
D = 1024
TOK = 1024
KC = D // P
TILES = TOK // P
BATCHES = 2
TPB = TILES // BATCHES
HALF = 512
NHALF = D // HALF
BLK = 32
NBLK = D // BLK
EXPERTS, RANK = 8, 16
ER = EXPERTS * RANK
AGW = ER + EXPERTS
SCALING = 32.0 / 16.0
EPS = 1e-5
FIRST = 3
RSQRT_MAGIC = float(0x5F3759DF)
CTX_CHUNKS = BATCHES * KC
CTX_PER_TILE = CTX_CHUNKS // (TILES - FIRST - 1)

F32 = mybir.dt.float32
F32R = mybir.dt.float32r
BF16 = mybir.dt.bfloat16
F16 = mybir.dt.float16
U8 = mybir.dt.uint8
I32 = mybir.dt.int32
U16 = mybir.dt.uint16
U32 = mybir.dt.uint32
ALU = mybir.AluOpType
ACT = mybir.ActivationFunctionType
AX_X = mybir.AxisListType.X
ds = bass.ds

STAT_STEPS = 3
LN_STEPS = 13
LN3_STEPS = 10
PAIR_GROUPS = TILES // 2
Q_MAX = 255.0
GATE_STEPS = 10


def decoder_layer(nc, xT_first, xT_rest, x_rows, ctx, wT, maskT, qparams, agT, baseT, base_b, lbT, consts, out):
    with ExitStack() as stack:
        def sb(name, cols, dt):
            return stack.enter_context(nc.sbuf_tensor(name, [P, cols], dt))

        def sem(name):
            return stack.enter_context(nc.semaphore(name))

        w_h = sb("w_h", KC * D, F32R)
        w_l = sb("w_l", KC * D, F32R)
        ctx_q = sb("ctx_q", BATCHES * KC * D, BF16)
        resid = sb("resid", TILES * D, F32)
        t_h = sb("t_h", 2 * D, F32R)
        t_l = sb("t_l", 2 * D, F32R)
        t_raw = sb("t_raw", 2 * D, F32)
        w_raw = sb("w_raw", 2 * D, F32)
        c_raw = sb("c_raw", 2 * D, F32)
        bias_row = sb("bias_row", D, F32)
        ctx_sum = sb("ctx_sum", BATCHES * D, F16)
        ctx_u16 = sb("ctx_u16", 2 * D, U16)
        q_u8 = sb("q_u8", 2 * D, U8)
        qT = sb("qT", 2 * D, BF16)
        const_sb = sb("const_sb", 2 * P + EXPERTS, F32)
        ident_bf = sb("ident_bf", P, BF16)
        ones_f16 = sb("ones_f16", P, F16)
        par = sb("par", 4, F32)
        par_u8 = sb("par_u8", 4, U8)
        derived = sb("derived", 16, F32)
        mask_rows_sb = sb("mask_rows_sb", 2 * NBLK, F32)
        bn = sb("bn", 12, F32)
        mean_var = sb("mean_var", 2 * TPB, F32)
        newton = sb("newton", 6 * TPB, F32)
        ln1_par = sb("ln1_par", 7 * 2, F32)
        ln2_par = sb("ln2_par", 2 * TILES, F32)
        ln3_par = sb("ln3_par", 2, F32)
        low_w = sb("low_w", ER, F32)
        lowT_h = sb("lowT_h", ER, F32R)
        lowT_l = sb("lowT_l", ER, F32R)
        top8 = sb("top8", 8, F32)
        top_i = sb("top_i", 8, U32)
        gate_logits = sb("gate_logits", EXPERTS, F32)
        gate = sb("gate", 8, F32)
        route = sb("route", 3 * EXPERTS, F32)
        with nc.sbuf_tensor("q_rows", [P, TILES * D], BF16) as q_rows:
            pass
        ag_h = sb("ag_h", KC * AGW, F32R)
        ag_l = sb("ag_l", KC * AGW, F32R)
        lb_h = sb("lb_h", D, F32R)
        lb_l = sb("lb_l", D, F32R)

        ps = stack.enter_context(nc.psum_tensor("ps", [P, 8 * HALF], F32))

        def bank(b, cols=HALF, at=0):
            return ps[:, b * HALF + at:b * HALF + at + cols]

        def acc(pair, n):
            return bank(2 * pair + n)

        def acc2(pair):
            return ps[:, pair * D:(pair + 1) * D]

        PAIR = (1, 0)
        SUMS = (6, 7)
        COLSUM = 2
        QT_PAIR = (2, 3)
        X2T_PAIR = 2
        LOGITS, LOWT = 6, 7

        rstd1, nmr1, q_scale, q_bias, row_sum, row_corr, shift1 = (ln1_par[:, 2 * i:2 * i + 2] for i in range(7))
        rstd2, nmr2 = ln2_par[:, 0:TILES], ln2_par[:, TILES:2 * TILES]

        ident = const_sb[:, 0:P]
        blockones = const_sb[:, P:2 * P]
        iota = const_sb[:, 2 * P:2 * P + EXPERTS]
        s12, z12 = par[:, 0:2], par[:, 2:4]
        z1, z2 = par[:, 2:3], par[:, 3:4]
        r12, r1, r2 = derived[:, 0:2], derived[:, 0:1], derived[:, 1:2]
        zi12, zi2 = derived[:, 2:4], derived[:, 3:4]
        neg_zi12, neg_zi1 = derived[:, 4:6], derived[:, 4:5]
        zf12, zf1, zf2 = derived[:, 6:8], derived[:, 6:7], derived[:, 7:8]
        ss, col_w, row_w, row_c = (derived[:, i:i + 1] for i in (8, 9, 10, 11))

        consts_loaded = sem("consts_loaded")
        params_loaded = sem("params_loaded")
        mask_loaded = [sem(f"mask_loaded{s}") for s in range(2)]
        w_loaded = [sem(f"w_loaded{s}") for s in range(2)]
        xchunk_loaded = [sem(f"xchunk_loaded{s}") for s in range(2)]
        xT_loaded = [sem(f"xT_loaded{s}") for s in range(2)]
        first_rows_loaded = [sem(f"first_rows_loaded{t}") for t in range(FIRST)]
        rows_loaded = [sem(f"rows_loaded{s}") for s in range(2)]
        ctx_loaded = [sem(f"ctx_loaded{s}") for s in range(2)]
        base_loaded = [sem(f"base_loaded{s}") for s in range(2)]
        ag_loaded = sem("ag_loaded")
        lb_loaded = sem("lb_loaded")
        bias_loaded = sem("bias_loaded")
        out_stored = sem("out_stored")
        par_step = sem("par_step")
        par_ready = sem("par_ready")
        consts_ready = sem("consts_ready")
        c_raw_read = sem("c_raw_read")
        block_sums = sem("block_sums")
        w_masked = sem("w_masked")
        w_hi = sem("w_hi")
        w_lo = sem("w_lo")
        xchunk_hi = sem("xchunk_hi")
        xchunk_lo = sem("xchunk_lo")
        chunk_done = sem("chunk_done")
        xT_hi = sem("xT_hi")
        xT_lo = sem("xT_lo")
        product_done = sem("product_done")
        acc_read = sem("acc_read")
        stat_step = sem("stat_step")
        ln_step = sem("ln_step")
        ln3_step = sem("ln3_step")
        q_par = sem("q_par")
        q_done = sem("q_done")
        q_rows_done = sem("q_rows_done")
        apply_step = sem("apply_step")
        x1_ready = sem("x1_ready")
        ctx_u16_free = sem("ctx_u16_free")
        ctx_sum_done = sem("ctx_sum_done")
        colsum_done = sem("colsum_done")
        corr_ready = sem("corr_ready")
        resid_added = sem("resid_added")
        q_transposed = sem("q_transposed")
        qT_ready = sem("qT_ready")
        small_hi = sem("small_hi")
        small_lo = sem("small_lo")
        x2_rows = sem("x2_rows")
        x2_transposed = sem("x2_transposed")
        x2T_hi = sem("x2T_hi")
        x2T_lo = sem("x2T_lo")
        logits_done = sem("logits_done")
        gate_step = sem("gate_step")
        gate_diff = sem("gate_diff")
        gate_exp = sem("gate_exp")
        low_ready = sem("low_ready")
        low_transposed = sem("low_transposed")
        lowT_hi = sem("lowT_hi")
        lowT_lo = sem("lowT_lo")
        half_done = sem("half_done")
        x3_ready = sem("x3_ready")

        def cols(tensor, i, width=D):
            return tensor[:, ds(i * width, width)]

        def xchunk_cols(slot):
            return slice(slot * FIRST * P, (slot + 1) * FIRST * P)

        def context_of(t):
            first = 2 + CTX_PER_TILE * (t - FIRST - 1)
            return range(first, min(first + CTX_PER_TILE, CTX_CHUNKS))

        block = stack.enter_context(nc.Block())

        @block.sync
        def _(sp):
            def load_mask(k, s):
                sp.dma_start(cols(c_raw, s).bitcast(I32), maskT[ds(k * P, P), :]).then_inc(mask_loaded[s], 16)

            def load_weights(k, s):
                sp.dma_start(cols(w_raw, s), wT[ds(k * P, P), :]).then_inc(w_loaded[s], 16)

            def load_xchunk(k, s):
                sp.dma_start(t_raw[:, xchunk_cols(s)], xT_first[ds(k * P, P), :]).then_inc(xchunk_loaded[s], 16)

            load_mask(0, 0)
            sp.dma_start(const_sb[:], consts).then_inc(consts_loaded, 16)
            load_weights(0, 0)
            load_xchunk(0, 0)
            load_mask(1, 1)
            load_weights(1, 1)
            load_xchunk(1, 1)
            sp.dma_start(par[:], qparams.partition_broadcast(P)).then_inc(params_loaded, 16)
            with sp.Fori(1, KC // 2) as j:
                for s in range(2):
                    k = 2 * j + s
                    sp.wait_ge(c_raw_read, k - 1)
                    load_mask(k, s)
                    sp.wait_ge(w_lo, k - 1)
                    load_weights(k, s)
                    sp.wait_ge(xchunk_lo, k - 1)
                    load_xchunk(k, s)

            def load_xT(t):
                sp.dma_start(cols(t_raw, t % 2), xT_rest[(t - FIRST) * P:(t - FIRST + 1) * P, :]).then_inc(xT_loaded[t % 2], 16)

            def load_rows(t, loaded):
                sp.dma_start(cols(resid, t), x_rows[t * P:(t + 1) * P, :]).then_inc(loaded, 16)

            def load_context(c):
                sp.wait_ge(c_raw_read, KC + c - 1)
                sp.dma_start(cols(c_raw, c % 2), ctx[c * P:(c + 1) * P, :]).then_inc(ctx_loaded[c % 2], 16)

            load_xT(FIRST)
            for t in range(FIRST):
                load_rows(t, first_rows_loaded[t])
            load_context(0)
            load_context(1)
            sp.wait_ge(xchunk_lo, KC)
            load_xT(FIRST + 1)
            for t in (FIRST, FIRST + 1):
                load_rows(t, rows_loaded[t % 2])
            for t in range(FIRST + 1, TILES):
                if t + 1 < TILES:
                    sp.wait_ge(xT_lo, t - FIRST)
                    load_xT(t + 1)
                if t > FIRST + 1:
                    sp.wait_ge(acc_read, t - 1)
                    load_rows(t, rows_loaded[t % 2])
                for c in context_of(t):
                    load_context(c)

            def load_base(k, s):
                sp.wait_ge(w_lo, KC + k - 1)
                sp.dma_start(cols(w_raw, s), baseT[ds(k * P, P), :]).then_inc(base_loaded[s], 16)

            load_base(0, 0)
            sp.wait_ge(w_lo, KC)
            load_base(1, 1)
            sp.wait_ge(c_raw_read, KC + BATCHES * KC)
            sp.dma_start(c_raw[:, 0:KC * AGW], agT).then_inc(ag_loaded, 16)
            sp.dma_start(bias_row[:], base_b.partition_broadcast(P)).then_inc(bias_loaded, 16)
            with sp.Fori(1, KC // 2) as j:
                for s in range(2):
                    load_base(2 * j + s, s)
            sp.wait_ge(w_lo, 2 * KC - 1)
            sp.dma_start(cols(w_raw, 0), lbT).then_inc(lb_loaded, 16)

            with sp.Fori(0, TILES - 1) as t:
                sp.wait_ge(x3_ready, t + 1)
                sp.dma_start(out[ds(t * P, P), :], cols(resid, t)).then_inc(out_stored, 16)
            for n in range(NHALF):
                sp.wait_ge(x3_ready, TILES + n)
                sp.dma_start(out[(TILES - 1) * P:, n * HALF:(n + 1) * HALF],
                             resid[:, (TILES - 1) * D + n * HALF:(TILES - 1) * D + (n + 1) * HALF]).then_inc(out_stored, 16)
            sp.wait_ge(out_stored, 16 * (TILES + 1))

        @block.vector
        def _(dve):
            def row_half_stats(n, row):
                dve.bn_stats(bn[:, 6 * n:6 * n + 6], row).then_inc(stat_step, 1)

            def row_stats(g):
                dve.drain()
                dve.bn_aggr(mean_var[:, 2 * g:2 * g + 2], bn[:]).then_inc(stat_step, 1)

            def row_params(group, tiles_done, width, rstd, nmr):
                base = group * LN_STEPS
                mean, var = (mean_var[:, 0:2 * width].rearrange("p (g c) -> p c g", c=2)[:, c, :] for c in range(2))
                v, minus_half_v, seed, second, third, t = (newton[:, TPB * i:TPB * i + width] for i in range(6))
                dve.wait_ge(stat_step, tiles_done * STAT_STEPS)
                dve.tensor_scalar(v, var, EPS, None, ALU.add).then_inc(ln_step, 1)
                dve.tensor_scalar(minus_half_v, var, EPS, -0.5, ALU.add, ALU.mult).then_inc(ln_step, 1)
                dve.wait_ge(ln_step, base + 1)
                dve.tensor_scalar(seed.bitcast(I32), v.bitcast(I32), -0.5, RSQRT_MAGIC, ALU.mult, ALU.add).then_inc(ln_step, 1)
                r = seed
                for n, new in enumerate((second, third, rstd)):
                    dve.wait_ge(ln_step, base + 3 + 3 * n)
                    dve.tensor_tensor(t, r, r, ALU.mult).then_inc(ln_step, 1)
                    dve.wait_ge(ln_step, base + 4 + 3 * n)
                    dve.tensor_tensor(t, t, minus_half_v, ALU.mult).then_inc(ln_step, 1)
                    dve.wait_ge(ln_step, base + 5 + 3 * n)
                    dve.scalar_tensor_tensor(new, t, 1.5, r, ALU.add, ALU.mult).then_inc(ln_step, 1)
                    r = new
                dve.wait_ge(ln_step, base + 12)
                dve.scalar_tensor_tensor(nmr, mean, -1.0, rstd, ALU.mult, ALU.mult).then_inc(ln_step, 1)

            def last_params(tile):
                base = tile * LN3_STEPS
                mean, var = mean_var[:, 0:1], mean_var[:, 1:2]
                v, minus_half_v, seed, second, third, t = (newton[:, i:i + 1] for i in range(6))
                dve.wait_ge(stat_step, (2 * TILES + tile + 1) * STAT_STEPS)
                dve.tensor_scalar(v, var, EPS, None, ALU.add).then_inc(ln3_step, 1)
                dve.tensor_scalar(minus_half_v, var, EPS, -0.5, ALU.add, ALU.mult).then_inc(ln3_step, 1)
                dve.wait_ge(ln3_step, base + 1)
                dve.tensor_scalar(seed.bitcast(I32), v.bitcast(I32), -0.5, RSQRT_MAGIC, ALU.mult, ALU.add).then_inc(ln3_step, 1)
                r = seed
                for n, new in enumerate((second, third, ln3_par[:, 0:1])):
                    dve.wait_ge(ln3_step, base + 3 + 2 * n)
                    dve.scalar_tensor_tensor(t, r, minus_half_v, r, ALU.mult, ALU.mult).then_inc(ln3_step, 1)
                    dve.wait_ge(ln3_step, base + 4 + 2 * n)
                    dve.scalar_tensor_tensor(new, t, 1.5, r, ALU.add, ALU.mult).then_inc(ln3_step, 1)
                    r = new
                dve.wait_ge(ln3_step, base + 9)
                dve.scalar_tensor_tensor(ln3_par[:, 1:2], mean, -1.0, r, ALU.mult, ALU.mult).then_inc(ln3_step, 1)

            def sum_mask_rows(s, loads):
                dve.wait_ge(mask_loaded[s], 16 * loads)
                dve.tensor_reduce(cols(mask_rows_sb, s, NBLK),
                                  cols(c_raw, s).bitcast(I32).rearrange("p (b c) -> p b c", c=BLK),
                                  AX_X, ALU.add).then_inc(c_raw_read, 1)

            def mask_chunk(k, s, loads, more=True):
                dve.wait_ge(block_sums, k + 1)
                dve.wait_ge(w_loaded[s], 16 * loads)
                w = cols(w_raw, s).rearrange("p (b c) -> p b c", c=BLK)
                sums = bank(SUMS[s], NBLK).unsqueeze(2).to_broadcast([P, NBLK, BLK])
                dve.scalar_tensor_tensor(w, sums, 0.0, w, ALU.is_gt, ALU.mult).then_inc(w_masked, 1)
                if more:
                    sum_mask_rows(1 - s, loads + s)

            sum_mask_rows(0, 1)
            with dve.Fori(0, KC // 2 - 1) as j:
                for s in range(2):
                    mask_chunk(2 * j + s, s, j + 1)
            mask_chunk(KC - 2, 0, KC // 2)
            mask_chunk(KC - 1, 1, KC // 2, more=False)

            dve.wait_ge(params_loaded, 16)
            dve.reciprocal(r12, s12).then_inc(par_step, 1)
            dve.tensor_copy(par_u8[:, 0:2], z12).then_inc(par_step, 1)
            dve.tensor_tensor(ss, par[:, 0:1], par[:, 1:2], ALU.mult).then_inc(par_step, 1)
            dve.wait_ge(par_step, 3)
            dve.tensor_copy(zi12, par_u8[:, 0:2]).then_inc(par_step, 1)
            dve.wait_ge(par_step, 4)
            dve.tensor_scalar(neg_zi12, zi12, -1.0, None, ALU.mult).then_inc(par_step, 1)
            dve.tensor_tensor(zf12, z12, zi12, ALU.subtract).then_inc(par_step, 1)
            dve.wait_ge(par_step, 6)
            dve.scalar_tensor_tensor(col_w, zf1, -1.0, ss, ALU.mult, ALU.mult).then_inc(par_step, 1)
            dve.scalar_tensor_tensor(row_w, zf2, -1.0, ss, ALU.mult, ALU.mult).then_inc(par_step, 1)
            dve.wait_ge(par_step, 8)
            dve.scalar_tensor_tensor(row_c, row_w, -float(D), zf1, ALU.mult, ALU.mult).then_inc(par_step, 1)
            dve.wait_ge(par_step, 9)
            dve.memset(ctx_u16[:, 0:1], 0.0).then_inc(ctx_u16_free, 2)
            dve.memset(ones_f16[:], 1.0).then_inc(par_ready, 1)
            dve.wait_ge(consts_loaded, 16)
            dve.tensor_copy(ident_bf[:], ident).then_inc(consts_ready, 1)

            def add_rows1(t, pair):
                dve.wait_ge(product_done, t + 1)
                dve.tensor_tensor(cols(resid, t), acc2(pair), cols(resid, t), ALU.add).then_inc(acc_read, 1)

            def tile_stats(t, g):
                dve.drain()
                for n in range(NHALF):
                    row_half_stats(n, resid[:, ds(t * D + n * HALF, HALF)])
                row_stats(g)

            def quant_params(c):
                row_params(c, 2 * c + 2, 2, rstd1, nmr1)
                dve.wait_ge(ln_step, (c + 1) * LN_STEPS)
                dve.tensor_scalar(q_scale, rstd1, r1, None, ALU.mult).then_inc(q_par, 1)
                dve.tensor_scalar(q_bias, nmr1, r1, z1, ALU.mult, ALU.add).then_inc(q_par, 1)

            def apply1(c):
                dve.wait_ge(q_rows_done, 2 * c + 2)
                dve.tensor_scalar(row_corr, row_sum, row_w, row_c, ALU.mult, ALU.add).then_inc(apply_step, 1)
                dve.wait_ge(apply_step, 2 * c + 1)
                dve.tensor_tensor(shift1, row_corr, nmr1, ALU.add).then_inc(apply_step, 1)
                dve.wait_ge(apply_step, 2 * c + 2)
                for g in range(2):
                    dve.tensor_scalar(cols(resid, 2 * c + g), cols(resid, 2 * c + g), rstd1[:, g:g + 1],
                                      shift1[:, g:g + 1], ALU.mult, ALU.add).then_inc(x1_ready, 1)

            def context_chunks(pair):
                for c in pair:
                    dve.wait_ge(c_raw_read, KC + c + 1)
                    dve.tensor_scalar(cols(ctx_q, c), cols(ctx_u16, c % 2), Q_MAX, zi2,
                                      ALU.min, ALU.subtract).then_inc(ctx_u16_free, 1)
                for c in pair:
                    b, nth = divmod(c, KC)
                    total = cols(ctx_sum, b)
                    if nth:
                        dve.wait_ge(ctx_u16_free, 2 + c + 1)
                        if nth > 1:
                            dve.wait_ge(ctx_sum_done, (KC - 1) * b + nth - 1)
                        dve.tensor_tensor(total, cols(ctx_q, c - 1) if nth == 1 else total,
                                          cols(ctx_q, c), ALU.add).then_inc(ctx_sum_done, 1)

            for t in range(2):
                dve.wait_ge(first_rows_loaded[t], 16)
                add_rows1(t, t)
            for t in range(2):
                tile_stats(t, t)
            quant_params(0)
            dve.wait_ge(first_rows_loaded[2], 16)
            add_rows1(2, 2)
            tile_stats(2, 0)
            context_chunks((0, 1))
            apply1(0)
            for t in range(FIRST + 1, TILES):
                dve.wait_ge(rows_loaded[(t - 1) % 2], 16 * ((t - FIRST + 1) // 2))
                add_rows1(t - 1, PAIR[(t - 1) % 2])
                tile_stats(t - 1, (t - 1) % 2)
                chunks = context_of(t)
                context_chunks(chunks[:2])
                if t % 2 == 0:
                    quant_params(t // 2 - 1)
                context_chunks(chunks[2:])
                if t % 2:
                    apply1((t - FIRST) // 2)
            dve.wait_ge(rows_loaded[1], 16 * 3)
            add_rows1(TILES - 1, PAIR[1])
            tile_stats(TILES - 1, 1)
            quant_params(3)

            def rows2(t, s, g):
                dve.wait_ge(resid_added, t + 1)
                dve.wait_ge(product_done, TILES + t + 1)
                dve.scalar_tensor_tensor(cols(resid, t), acc2(PAIR[s]), ss, cols(resid, t),
                                         ALU.mult, ALU.add).then_inc(acc_read, 1)
                tile_stats(t, g)

            def split_x2T(t, s):
                for n in range(NHALF):
                    dve.wait_ge(x2T_hi, NHALF * t + n + 1)
                    dve.tensor_tensor(t_l[:, s * D + n * HALF:s * D + (n + 1) * HALF], acc(X2T_PAIR, n),
                                      t_h[:, s * D + n * HALF:s * D + (n + 1) * HALF].bitcast(F32),
                                      ALU.subtract).then_inc(x2T_lo, 1)

            def batch_params(b):
                row_params(PAIR_GROUPS + b, TILES + (b + 1) * TPB, TPB,
                           rstd2[:, b * TPB:(b + 1) * TPB], nmr2[:, b * TPB:(b + 1) * TPB])

            rows2(0, 0, 0)
            rows2(1, 1, 1)
            apply1(3)
            rows2(2, 0, 2)
            rows2(3, 1, 3)
            batch_params(0)
            for t in range(TPB, TILES - 1):
                rows2(t, t % 2, t - TPB)
            split_x2T(0, 0)
            rows2(TILES - 1, 1, TPB - 1)
            batch_params(1)

            def route_tokens(t):
                base = t * GATE_STEPS
                dve.wait_ge(logits_done, t + 1)
                dve.tensor_copy(gate_logits[:], bank(LOGITS, EXPERTS, at=ER)).then_inc(gate_step, 1)
                dve.drain()
                dve.max(top8[:], gate_logits[:]).then_inc(gate_step, 1)
                dve.wait_ge(gate_step, base + 2)
                dve.tensor_tensor(gate[:, 0:1], top8[:, 1:2], top8[:, 0:1], ALU.subtract).then_inc(gate_diff, 1)
                dve.max_index(top_i[:], top8[:], gate_logits[:]).then_inc(gate_step, 1)
                dve.wait_ge(gate_step, base + 3)
                dve.tensor_copy(gate[:, 2:4], top_i[:, 0:2]).then_inc(gate_step, 1)
                dve.wait_ge(gate_exp, t + 1)
                dve.tensor_scalar(gate[:, 4:5], gate[:, 1:2], 1.0, None, ALU.add).then_inc(gate_step, 1)
                dve.wait_ge(gate_step, base + 5)
                dve.reciprocal(gate[:, 5:6], gate[:, 4:5]).then_inc(gate_step, 1)
                dve.wait_ge(gate_step, base + 6)
                dve.tensor_tensor(gate[:, 6:7], gate[:, 1:2], gate[:, 5:6], ALU.mult).then_inc(gate_step, 1)
                dve.tensor_scalar(route[:, 0:EXPERTS], iota, gate[:, 2:3], gate[:, 5:6],
                                  ALU.is_equal, ALU.mult).then_inc(gate_step, 1)
                dve.wait_ge(gate_step, base + 7)
                dve.tensor_scalar(route[:, EXPERTS:2 * EXPERTS], iota, gate[:, 3:4], gate[:, 6:7],
                                  ALU.is_equal, ALU.mult).then_inc(gate_step, 1)
                dve.wait_ge(gate_step, base + 9)
                dve.tensor_tensor(route[:, 2 * EXPERTS:], route[:, 0:EXPERTS], route[:, EXPERTS:2 * EXPERTS],
                                  ALU.add).then_inc(gate_step, 1)
                dve.wait_ge(gate_step, base + 10)
                dve.scalar_tensor_tensor(low_w[:].rearrange("p (e r) -> p e r", r=RANK),
                                         bank(LOGITS, ER).rearrange("p (e r) -> p e r", r=RANK), SCALING,
                                         route[:, 2 * EXPERTS:].unsqueeze(2).to_broadcast([P, EXPERTS, RANK]),
                                         ALU.mult, ALU.mult).then_inc(low_ready, 1)

            def mixture_rows(t, s, more=True):
                route_tokens(t)
                dve.wait_ge(lowT_hi, t + 1)
                dve.tensor_tensor(lowT_l[:], bank(LOWT, P), lowT_h[:].bitcast(F32), ALU.subtract).then_inc(lowT_lo, 1)
                if more:
                    split_x2T(t + 1, 1 - s)
                halves = [resid[:, ds(t * D + n * HALF, HALF)] for n in range(NHALF)]
                dve.wait_ge(resid_added, TILES + t + 1)
                dve.wait_ge(half_done, t + 1)
                dve.tensor_tensor(halves[0], acc(PAIR[s], 0), halves[0], ALU.add)
                dve.drain()
                row_half_stats(0, halves[0])
                dve.wait_ge(product_done, 2 * TILES + t + 1)
                dve.tensor_tensor(halves[1], acc(PAIR[s], 1), halves[1], ALU.add).then_inc(acc_read, 1)
                dve.drain()
                row_half_stats(1, halves[1])
                row_stats(0)
                last_params(t)
                dve.wait_ge(ln3_step, (t + 1) * LN3_STEPS)
                for part in [cols(resid, t)] if more else halves:
                    dve.tensor_scalar(part, part, ln3_par[:, 0:1], ln3_par[:, 1:2],
                                      ALU.mult, ALU.add).then_inc(x3_ready, 1)

            with dve.Fori(0, TILES // 2 - 1) as j:
                for s in range(2):
                    mixture_rows(2 * j + s, s)
            mixture_rows(TILES - 2, 0)
            mixture_rows(TILES - 1, 1, more=False)

        @block.scalar
        def _(act):
            def round_chunk(k, s, loads, reuse):
                act.wait_ge(xchunk_loaded[s], 16 * loads)
                if reuse:
                    act.wait_ge(chunk_done, k - 1)
                nc.scalar.activation(t_h[:, xchunk_cols(s)], t_raw[:, xchunk_cols(s)], ACT.Copy).then_inc(xchunk_hi, 1)
                act.wait_ge(w_masked, k + 1)
                nc.scalar.activation(cols(w_h, k), cols(w_raw, s), ACT.Copy).then_inc(w_hi, 1)

            round_chunk(0, 0, 1, False)
            round_chunk(1, 1, 1, False)
            with act.Fori(1, KC // 2) as j:
                for s in range(2):
                    round_chunk(2 * j + s, s, j + 1, True)

            def round_xT(t):
                act.wait_ge(xT_loaded[t % 2], 16 * ((t - FIRST) // 2 + 1))
                if t > FIRST:
                    act.wait_ge(product_done, t - 1)
                nc.scalar.activation(cols(t_h, t % 2), cols(t_raw, t % 2), ACT.Copy).then_inc(xT_hi, 1)

            round_xT(FIRST)
            round_xT(FIRST + 1)

            def quantise_rows(t, s):
                nc.scalar.activation(cols(q_u8, s), cols(resid, t), ACT.Identity, bias=q_bias[:, s:s + 1],
                                     scale=q_scale[:, s:s + 1]).then_inc(q_done, 1)
                act.wait_ge(q_done, t + 1)
                nc.scalar.activation(cols(q_rows, t), cols(q_u8, s), ACT.Identity, bias=neg_zi1,
                                     accum_out=row_sum[:, s:s + 1]).then_inc(q_rows_done, 1)

            def quantise_pair(c):
                act.wait_ge(q_par, 2 * c + 2)
                for s in range(2):
                    quantise_rows(2 * c + s, s)

            def quantise_context(pair):
                for c in pair:
                    act.wait_ge(ctx_loaded[c % 2], 16 * (c // 2 + 1))
                    act.wait_ge(ctx_u16_free, c + 1)
                    nc.scalar.activation(cols(ctx_u16, c % 2), cols(c_raw, c % 2), ACT.Identity, bias=z2,
                                         scale=r2).then_inc(c_raw_read, 1)

            act.wait_ge(par_ready, 1)
            quantise_context((0, 1))
            quantise_pair(0)
            for t in range(FIRST + 1, TILES - 1):
                round_xT(t + 1)
                quantise_context(context_of(t))
                if t % 2 == 0:
                    quantise_pair(t // 2 - 1)

            def column_correction(b):
                act.wait_ge(colsum_done, b + 1)
                act.wait_ge(xT_lo, TILES - FIRST - 1 + b)
                nc.scalar.activation(cols(t_raw, b), acc2(COLSUM), ACT.Copy, scale=col_w).then_inc(corr_ready, 1)

            def copy_qT(t):
                act.wait_ge(q_transposed, t + 1)
                if t >= 2:
                    act.wait_ge(product_done, TILES + t - 1)
                nc.scalar.activation(cols(qT, t % 2), acc2(QT_PAIR[t % 2] if t else QT_PAIR[1]),
                                     ACT.Copy).then_inc(qT_ready, 1)

            def round_base(k):
                if k == 0:
                    act.wait_ge(product_done, TILES)
                act.wait_ge(base_loaded[k % 2], 16 * (k // 2 + 1))
                nc.scalar.activation(cols(w_h, k), cols(w_raw, k % 2), ACT.Copy).then_inc(w_hi, 1)

            def normalise2(t, s):
                nc.scalar.activation(cols(t_raw, s), cols(resid, t), ACT.Identity, bias=cols(nmr2, t, 1),
                                     scale=cols(rstd2, t, 1)).then_inc(x2_rows, 1)

            def round_x2T(t, s):
                act.wait_ge(product_done, 2 * TILES + t - 1)
                for n in range(NHALF):
                    act.wait_ge(x2_transposed, NHALF * t + n + 1)
                    nc.scalar.activation(t_h[:, s * D + n * HALF:s * D + (n + 1) * HALF], acc(X2T_PAIR, n),
                                         ACT.Copy).then_inc(x2T_hi, 1)

            copy_qT(0)
            column_correction(0)
            quantise_context(context_of(TILES - 1))
            copy_qT(1)
            column_correction(1)
            round_base(0)
            round_base(1)
            copy_qT(2)
            quantise_pair(3)
            for k in range(2, KC - 2):
                copy_qT(k + 1)
                round_base(k)
            act.wait_ge(ln_step, (PAIR_GROUPS + 1) * LN_STEPS)
            act.wait_ge(resid_added, TPB)
            normalise2(0, 0)
            copy_qT(TILES - 1)
            act.wait_ge(q_transposed, TILES)
            act.wait_ge(ag_loaded, 16)
            nc.scalar.activation(ag_h[:], c_raw[:, 0:KC * AGW], ACT.Copy).then_inc(small_hi, 1)
            round_base(KC - 2)
            round_x2T(0, 0)
            round_base(KC - 1)
            act.wait_ge(resid_added, TILES)
            normalise2(1, 1)
            act.wait_ge(lb_loaded, 16)
            nc.scalar.activation(lb_h[:], cols(w_raw, 0), ACT.Copy).then_inc(small_hi, 1)

            def mixture_tile(t, s, left):
                act.wait_ge(gate_diff, t + 1)
                nc.scalar.activation(gate[:, 1:2], gate[:, 0:1], ACT.Exp).then_inc(gate_exp, 1)
                act.wait_ge(low_transposed, t + 1)
                nc.scalar.activation(lowT_h[:], bank(LOWT, P), ACT.Copy).then_inc(lowT_hi, 1)
                if left >= 1:
                    round_x2T(t + 1, 1 - s)
                if left >= 2:
                    act.wait_ge(ln_step, (PAIR_GROUPS + 2) * LN_STEPS)
                    act.wait_ge(resid_added, TILES + t + 1)
                    normalise2(t + 2, s)

            with act.Fori(0, TILES // 2 - 1) as j:
                for s in range(2):
                    mixture_tile(2 * j + s, s, 2)
            mixture_tile(TILES - 2, 0, 1)
            mixture_tile(TILES - 1, 1, 0)

        @block.gpsimd
        def _(pool):
            def low_part(out, raw, high):
                return pool.tensor_tensor(out, raw, high.bitcast(F32), ALU.subtract)

            def split_weights(nth, k, s):
                pool.wait_ge(w_hi, nth + 1)
                low_part(cols(w_l, k), cols(w_raw, s), cols(w_h, k)).then_inc(w_lo, 1)

            def split_xchunk(k, s):
                pool.wait_ge(xchunk_hi, k + 1)
                low_part(t_l[:, xchunk_cols(s)], t_raw[:, xchunk_cols(s)], t_h[:, xchunk_cols(s)]).then_inc(xchunk_lo, 1)

            with pool.Fori(0, KC // 2) as j:
                for s in range(2):
                    k = 2 * j + s
                    split_xchunk(k, s)
                    split_weights(k, k, s)

            pool.wait_ge(xT_hi, 1)
            low_part(cols(t_l, 1), cols(t_raw, 1), cols(t_h, 1)).then_inc(xT_lo, 1)
            with pool.Fori(2, TILES // 2) as j:
                for s in range(2):
                    t = 2 * j + s
                    pool.wait_ge(xT_hi, t - FIRST + 1)
                    low_part(cols(t_l, s), cols(t_raw, s), cols(t_h, s)).then_inc(xT_lo, 1)

            def add_correction(t, b):
                pool.wait_ge(x1_ready, t + 1)
                pool.tensor_tensor(cols(resid, t), cols(resid, t), cols(t_raw, b), ALU.add).then_inc(resid_added, 1)

            pool.wait_ge(corr_ready, 1)
            with pool.Fori(0, TPB) as t:
                add_correction(t, 0)
            pool.wait_ge(corr_ready, 2)
            with pool.Fori(0, TPB // 2) as j:
                for s in range(2):
                    k = 2 * j + s
                    split_weights(KC + k, k, s)
                    add_correction(TPB + k, 1)
            split_weights(KC + TPB, TPB, 0)
            split_weights(KC + TPB + 1, TPB + 1, 1)
            pool.wait_ge(small_hi, 1)
            low_part(ag_l[:], c_raw[:, 0:KC * AGW], ag_h[:]).then_inc(small_lo, 1)
            split_weights(KC + TPB + 2, TPB + 2, 0)
            split_weights(KC + TPB + 3, TPB + 3, 1)
            pool.wait_ge(small_hi, 2)
            low_part(lb_l[:], cols(w_raw, 0), lb_h[:]).then_inc(small_lo, 1)

            pool.wait_ge(bias_loaded, 16)
            with pool.Fori(0, TILES // 2) as j:
                for s in range(2):
                    t = 2 * j + s
                    pool.wait_ge(x2_rows, t + 1)
                    pool.tensor_tensor(cols(resid, t), cols(t_raw, s), bias_row[:], ALU.add).then_inc(resid_added, 1)

        @block.tensor
        def _(pe):
            def w_half(tensor, k, n):
                return tensor[:, ds(k * D + n * HALF, HALF)]

            def sum_mask_blocks(k, s):
                pe.wait_ge(c_raw_read, k + 1)
                pe.matmul(bank(SUMS[s], NBLK), blockones, cols(mask_rows_sb, s, NBLK),
                          start=True, stop=True).then_inc(block_sums, 1)

            def chunk_cols(s, t):
                return slice((s * FIRST + t) * P, (s * FIRST + t + 1) * P)

            def chunk_products(k, s, start=False, stop=False):
                if not start and not stop:
                    sum_mask_blocks(k + 1, 1 - s)
                pe.wait_ge(w_hi, k + 1)
                for t in range(FIRST):
                    for n in range(NHALF):
                        pe.matmul(acc(t, n), t_h[:, chunk_cols(s, t)], w_half(w_h, k, n), start=start, stop=False)
                if start:
                    sum_mask_blocks(k + 1, 1 - s)
                pe.wait_ge(xchunk_lo, k + 1)
                pe.wait_ge(w_lo, k + 1)
                for t in range(FIRST):
                    for n in range(NHALF):
                        pe.matmul(acc(t, n), t_l[:, chunk_cols(s, t)], w_half(w_h, k, n), start=False, stop=False)
                        last = pe.matmul(acc(t, n), t_h[:, chunk_cols(s, t)], w_half(w_l, k, n),
                                         start=False, stop=stop)
                    if stop:
                        last.then_inc(product_done, 1)
                if not stop:
                    last.then_inc(chunk_done, 1)

            pe.wait_ge(consts_loaded, 16)
            sum_mask_blocks(0, 0)
            chunk_products(0, 0, start=True)
            chunk_products(1, 1)
            with pe.Fori(1, KC // 2 - 1) as j:
                for s in range(2):
                    chunk_products(2 * j + s, s)
            chunk_products(KC - 2, 0)
            chunk_products(KC - 1, 1, stop=True)

            def split_product(s, n, chunks, stop):
                for k in chunks:
                    hi = t_h[:, s * D + k * P:s * D + (k + 1) * P]
                    lo = t_l[:, s * D + k * P:s * D + (k + 1) * P]
                    pe.matmul(acc(PAIR[s], n), hi, w_half(w_h, k, n), start=(k == 0), stop=False)
                    pe.matmul(acc(PAIR[s], n), hi, w_half(w_l, k, n), start=False, stop=False)
                    last = pe.matmul(acc(PAIR[s], n), lo, w_half(w_h, k, n), start=False, stop=(stop and k == KC - 1))
                return last

            def stage1_tile(t, s, reads):
                pe.wait_ge(acc_read, reads)
                pe.wait_ge(xT_hi, t - FIRST + 1)
                pe.wait_ge(xT_lo, t - FIRST + 1)
                for n in range(NHALF):
                    last = split_product(s, n, range(KC), True)
                last.then_inc(product_done, 1)

            with pe.Fori(1, TILES // 2 - 1) as j:
                stage1_tile(2 * j + 1, 1, 3 * j - 2)
                stage1_tile(2 * j + 2, 0, 2 * j + 1)

            def column_sums(b):
                pe.wait_ge(ctx_sum_done, (KC - 1) * (b + 1))
                for n in range(NHALF):
                    last = pe.matmul(acc(COLSUM, n), ones_f16[:], ctx_sum[:, b * D + n * HALF:b * D + (n + 1) * HALF],
                                     start=True, stop=True)
                last.then_inc(colsum_done, 1)

            def transpose_q(t, pair):
                pe.wait_ge(q_rows_done, t + 1)
                for k in range(KC):
                    last = pe.matmul(ps[:, pair * D + k * P:pair * D + (k + 1) * P],
                                     q_rows[:, ds(t * D + k * P, P)], ident_bf[:], start=True, stop=True,
                                     skip_group_check=True)
                last.then_inc(q_transposed, 1)

            def stage2_product(t, s, b):
                pe.wait_ge(qT_ready, t + 1)
                pe.wait_ge(acc_read, TILES + t - 1)
                for n in range(NHALF):
                    for k in range(KC):
                        last = pe.matmul(acc(PAIR[s], n), qT[:, s * D + k * P:s * D + (k + 1) * P],
                                         w_half(ctx_q, b * KC + k, n), start=(k == 0), stop=(k == KC - 1))
                last.then_inc(product_done, 1)

            pe.wait_ge(par_ready, 1)
            pe.wait_ge(consts_ready, 1)
            transpose_q(0, QT_PAIR[1])
            pe.wait_ge(acc_read, FIRST)
            column_sums(0)
            stage1_tile(TILES - 1, 1, TILES - 2)
            pe.wait_ge(qT_ready, 1)
            transpose_q(1, QT_PAIR[1])
            pe.wait_ge(corr_ready, 1)
            column_sums(1)
            with pe.Fori(0, TPB // 2) as j:
                stage2_product(2 * j, 0, 0)
                pe.wait_ge(corr_ready, 2)
                transpose_q(2 * j + 2, QT_PAIR[0])
                stage2_product(2 * j + 1, 1, 0)
                transpose_q(2 * j + 3, QT_PAIR[1])
            stage2_product(4, 0, 1)
            transpose_q(6, QT_PAIR[0])
            stage2_product(5, 1, 1)
            transpose_q(7, QT_PAIR[1])
            stage2_product(6, 0, 1)

            def transpose_x2(t, s):
                pe.wait_ge(x2_rows, t + 1)
                for n in range(NHALF):
                    for k in range(n * KC // 2, (n + 1) * KC // 2):
                        last = pe.transpose(ps[:, X2T_PAIR * D + k * P:X2T_PAIR * D + (k + 1) * P],
                                            t_raw[:, s * D + k * P:s * D + (k + 1) * P], ident)
                    last.then_inc(x2_transposed, 1)

            def low_and_logits(t, s):
                pe.wait_ge(x2T_hi, NHALF * (t + 1))
                pe.wait_ge(x2T_lo, NHALF * (t + 1))
                for k in range(KC):
                    hi = t_h[:, s * D + k * P:s * D + (k + 1) * P]
                    lo = t_l[:, s * D + k * P:s * D + (k + 1) * P]
                    high, low = (a[:, k * AGW:(k + 1) * AGW] for a in (ag_h, ag_l))
                    pe.matmul(bank(LOGITS, AGW), hi, high, start=(k == 0), stop=False)
                    pe.matmul(bank(LOGITS, AGW), hi, low, start=False, stop=False)
                    last = pe.matmul(bank(LOGITS, AGW), lo, high, start=False, stop=(k == KC - 1))
                last.then_inc(logits_done, 1)

            def lora_product(s, n):
                half = slice(n * HALF, (n + 1) * HALF)
                pe.matmul(acc(PAIR[s], n), lowT_h[:], lb_h[:, half], start=False, stop=False)
                pe.matmul(acc(PAIR[s], n), lowT_h[:], lb_l[:, half], start=False, stop=False)
                return pe.matmul(acc(PAIR[s], n), lowT_l[:], lb_h[:, half], start=False, stop=True)

            def stage3_tile(t, s, more=True):
                low_and_logits(t, s)
                pe.wait_ge(w_lo, 2 * KC)
                pe.wait_ge(acc_read, 2 * TILES + t - 1)
                split_product(s, 0, range(KC), False)
                pe.wait_ge(low_ready, t + 1)
                pe.transpose(bank(LOWT, P), low_w[:], ident).then_inc(low_transposed, 1)
                if more:
                    transpose_x2(t + 1, 1 - s)
                split_product(s, 1, range(KC // 2), False)
                pe.wait_ge(lowT_hi, t + 1)
                pe.wait_ge(lowT_lo, t + 1)
                pe.wait_ge(small_lo, 2)
                lora_product(s, 0).then_inc(half_done, 1)
                split_product(s, 1, range(KC // 2, KC), False)
                lora_product(s, 1).then_inc(product_done, 1)

            transpose_x2(0, 0)
            stage2_product(TILES - 1, 1, 1)
            pe.wait_ge(small_lo, 1)
            with pe.Fori(0, TILES // 2 - 1) as j:
                for s in range(2):
                    stage3_tile(2 * j + s, s)
            stage3_tile(TILES - 2, 0)
            stage3_tile(TILES - 1, 1, more=False)


def kernel(**inputs):
    import numpy as np
    import concourse.bacc as bacc
    from concourse.bass_utils import run_bass_kernel_spmd

    def arr(name):
        return np.asarray(inputs[name])

    x_rows = arr("x").reshape(TOK, D)
    rows = np.arange(P)
    consts = np.concatenate([np.eye(P), (rows[:, None] // BLK == rows[None, :] // BLK),
                             np.broadcast_to(np.arange(EXPERTS), (P, EXPERTS))], axis=1).astype(np.float32)
    laid_out = {
        "xT_first": x_rows[:FIRST * P].T,
        "xT_rest": x_rows[FIRST * P:].reshape(TILES - FIRST, P, KC, P).transpose(0, 3, 2, 1).reshape(-1, D),
        "x_rows": x_rows,
        "ctx": arr("ctx_4096").reshape(BATCHES * D, D),
        "wT": arr("L0_attn_weight").T,
        "maskT": arr("L0_attn_mask").T,
        "qparams": np.concatenate([arr("L0_xattn_x1_scale"), arr("L0_xattn_x2_scale"),
                                   arr("L0_xattn_x1_zp"), arr("L0_xattn_x2_zp")]),
        "agT": np.concatenate([arr("L0_ffn_lora_A").reshape(ER, D), arr("L0_ffn_gate_w")], axis=0)
                 .T.reshape(KC, P, AGW).transpose(1, 0, 2).reshape(P, KC * AGW),
        "baseT": arr("L0_ffn_base_w").T,
        "base_b": arr("L0_ffn_base_b"),
        "lbT": arr("L0_ffn_lora_B").transpose(0, 2, 1).reshape(ER, D),
        "consts": consts,
    }
    nc = bacc.Bacc("TRN2", target_bir_lowering=False, num_devices=1)
    arrays, args = {}, []
    for name, a in laid_out.items():
        a = np.ascontiguousarray(a)
        arrays[f"in_{name}"] = a
        args.append(nc.dram_tensor(f"in_{name}", a.shape, mybir.dt.from_np(a.dtype), kind="ExternalInput").ap())
    out = nc.dram_tensor("out", (TOK, D), F32, kind="ExternalOutput").ap()
    decoder_layer(nc, *args, out)
    result = run_bass_kernel_spmd(nc, [arrays], core_ids=[0])
    return result.results[0]["out"].reshape(BATCHES, TOK // BATCHES, D)
```

```python
from contextlib import ExitStack

import concourse.bass as bass
from concourse import mybir

P = 128
D = 1024
TOK = 1024
KC = D // P
TILES = TOK // P
BATCHES = 2
TPB = TILES // BATCHES
HALF = 512
NHALF = D // HALF
BLK = 32
NBLK = D // BLK
EXPERTS, RANK = 8, 16
ER = EXPERTS * RANK
AGW = ER + EXPERTS
SCALING = 32.0 / 16.0
EPS = 1e-5
FIRST = 3
RSQRT_MAGIC = float(0x5F3759DF)
CTX_CHUNKS = BATCHES * KC
CTX_PER_TILE = CTX_CHUNKS // (TILES - FIRST - 1)

F32 = mybir.dt.float32
F32R = mybir.dt.float32r
BF16 = mybir.dt.bfloat16
F16 = mybir.dt.float16
U8 = mybir.dt.uint8
I32 = mybir.dt.int32
U16 = mybir.dt.uint16
U32 = mybir.dt.uint32
ALU = mybir.AluOpType
ACT = mybir.ActivationFunctionType
AX_X = mybir.AxisListType.X
ds = bass.ds

MASK_STEPS = 3
STAT_STEPS = 3
LN_STEPS = 13
LN3_STEPS = 10
PAIR_GROUPS = TILES // 2
Q_MAX = 255.0
GATE_STEPS = 11


def decoder_layer(nc, xT_first, xT_rest, x_rows, ctx, wT, maskT, qparams, agT, baseT, base_b, lbT, consts, out):
    with ExitStack() as stack:
        def sb(name, cols, dt):
            return stack.enter_context(nc.sbuf_tensor(name, [P, cols], dt))

        def sem(name):
            return stack.enter_context(nc.semaphore(name))

        w_h = sb("w_h", KC * D, F32R)
        w_l = sb("w_l", KC * D, F32R)
        ctx_q = sb("ctx_q", BATCHES * KC * D, BF16)
        resid = sb("resid", TILES * D, F32)
        t_h = sb("t_h", 2 * D, F32R)
        t_l = sb("t_l", 2 * D, F32R)
        t_raw = sb("t_raw", 2 * D, F32)
        w_raw = sb("w_raw", 2 * D, F32)
        c_raw = sb("c_raw", 2 * D, F32)
        bias_row = sb("bias_row", D, F32)
        ctx_sum = sb("ctx_sum", BATCHES * D, F16)
        ctx_u16 = sb("ctx_u16", 2 * D, U16)
        q_u8 = sb("q_u8", 2 * D, U8)
        qT = sb("qT", 2 * D, BF16)
        const_sb = sb("const_sb", P + EXPERTS, F32)
        ident_bf = sb("ident_bf", P, BF16)
        ones_f16 = sb("ones_f16", P, F16)
        par = sb("par", 4, F32)
        par_u8 = sb("par_u8", 4, U8)
        derived = sb("derived", 16, F32)
        row_sums = sb("row_sums", NBLK, F32)
        row_sums_T = sb("row_sums_T", BLK, F32)
        block_sum = sb("block_sum", 1, F32)
        block_sums = sb("block_sums", NBLK, F32)
        bn = sb("bn", 12, F32)
        mean_var = sb("mean_var", 2 * TPB, F32)
        newton = sb("newton", 6 * TPB, F32)
        ln1_par = sb("ln1_par", 7 * 2, F32)
        ln2_par = sb("ln2_par", 2 * TILES, F32)
        ln3_par = sb("ln3_par", 2, F32)
        low_w = sb("low_w", ER, F32)
        lowT_h = sb("lowT_h", ER, F32R)
        lowT_l = sb("lowT_l", ER, F32R)
        top8 = sb("top8", 8, F32)
        top_i = sb("top_i", 8, U32)
        low_logits = sb("low_logits", AGW, F32)
        gate = sb("gate", 8, F32)
        route = sb("route", 3 * EXPERTS, F32)
        with nc.sbuf_tensor("q_rows", [P, TILES * D], BF16) as q_rows:
            pass
        ag_hl = sb("ag_hl", KC * 2 * AGW, F32R)
        lb_h = sb("lb_h", D, F32R)
        lb_l = sb("lb_l", D, F32R)

        ps = stack.enter_context(nc.psum_tensor("ps", [P, 8 * HALF], F32))

        def bank(b, cols=HALF, at=0):
            return ps[:, b * HALF + at:b * HALF + at + cols]

        def acc(pair, n):
            return bank(2 * pair + n)

        def acc2(pair):
            return ps[:, pair * D:(pair + 1) * D]

        PAIR = (1, 0)
        COLSUM = 2
        QT_PAIR = (2, 3)
        X2T_PAIR = 2
        LOGITS, LOWT = 6, 7

        rstd1, nmr1, q_scale, q_bias, row_sum, row_corr, shift1 = (ln1_par[:, 2 * i:2 * i + 2] for i in range(7))
        rstd2, nmr2 = ln2_par[:, 0:TILES], ln2_par[:, TILES:2 * TILES]

        ident = const_sb[:, 0:P]
        ag_high, ag_low = (ag_hl[:].rearrange("p (k h c) -> p h k c", h=2, c=AGW)[:, h] for h in range(2))
        ag_raw = c_raw[:, 0:KC * AGW].rearrange("p (k c) -> p k c", c=AGW)
        w_stage = ctx_q[:].bitcast(F32)
        iota = const_sb[:, P:P + EXPERTS]
        s12, z12 = par[:, 0:2], par[:, 2:4]
        z1, z2 = par[:, 2:3], par[:, 3:4]
        r12, r1, r2 = derived[:, 0:2], derived[:, 0:1], derived[:, 1:2]
        zi12, zi2 = derived[:, 2:4], derived[:, 3:4]
        neg_zi12, neg_zi1 = derived[:, 4:6], derived[:, 4:5]
        zf12, zf1, zf2 = derived[:, 6:8], derived[:, 6:7], derived[:, 7:8]
        ss, col_w, row_w, row_c = (derived[:, i:i + 1] for i in (8, 9, 10, 11))

        consts_loaded = sem("consts_loaded")
        params_loaded = sem("params_loaded")
        first_mask_loaded = [sem(f"first_mask_loaded{n}") for n in range(NHALF)]
        first_w_loaded = [sem(f"first_w_loaded{n}") for n in range(NHALF)]
        mask_loaded = [sem(f"mask_loaded{s}") for s in range(2)]
        w_loaded = [sem(f"w_loaded{s}") for s in range(2)]
        xchunk_loaded = [sem(f"xchunk_loaded{s}") for s in range(2)]
        xT_loaded = [sem(f"xT_loaded{s}") for s in range(2)]
        first_rows_loaded = [sem(f"first_rows_loaded{t}") for t in range(FIRST)]
        rows_loaded = [sem(f"rows_loaded{s}") for s in range(2)]
        ctx_loaded = [sem(f"ctx_loaded{s}") for s in range(2)]
        base_loaded = [sem(f"base_loaded{s}") for s in range(2)]
        ag_loaded = sem("ag_loaded")
        lb_loaded = sem("lb_loaded")
        bias_loaded = sem("bias_loaded")
        out_stored = sem("out_stored")
        par_step = sem("par_step")
        par_ready = sem("par_ready")
        consts_ready = sem("consts_ready")
        c_raw_read = sem("c_raw_read")
        mask_step = sem("mask_step")
        half_summed = sem("half_summed")
        half_masked = sem("half_masked")
        half_hi = sem("half_hi")
        half_lo = sem("half_lo")
        w_masked = sem("w_masked")
        w_hi = sem("w_hi")
        w_lo = sem("w_lo")
        xchunk_hi = sem("xchunk_hi")
        xchunk_lo = sem("xchunk_lo")
        chunk_done = sem("chunk_done")
        xT_hi = sem("xT_hi")
        xT_lo = sem("xT_lo")
        product_done = sem("product_done")
        acc_read = sem("acc_read")
        stat_step = sem("stat_step")
        ln_step = sem("ln_step")
        ln3_step = sem("ln3_step")
        q_par = sem("q_par")
        q_done = sem("q_done")
        q_rows_done = sem("q_rows_done")
        apply_step = sem("apply_step")
        x1_ready = sem("x1_ready")
        ctx_u16_free = sem("ctx_u16_free")
        ctx_sum_done = sem("ctx_sum_done")
        colsum_done = sem("colsum_done")
        corr_ready = sem("corr_ready")
        resid_added = sem("resid_added")
        q_transposed = sem("q_transposed")
        qT_ready = sem("qT_ready")
        small_hi = sem("small_hi")
        small_lo = sem("small_lo")
        x2_rows = sem("x2_rows")
        x2_transposed = sem("x2_transposed")
        x2T_hi = sem("x2T_hi")
        x2T_lo = sem("x2T_lo")
        logits_done = sem("logits_done")
        gate_step = sem("gate_step")
        gate_diff = sem("gate_diff")
        gate_exp = sem("gate_exp")
        low_ready = sem("low_ready")
        low_transposed = sem("low_transposed")
        lowT_hi = sem("lowT_hi")
        lowT_lo = sem("lowT_lo")
        half_done = sem("half_done")
        x3_ready = sem("x3_ready")

        def cols(tensor, i, width=D):
            return tensor[:, ds(i * width, width)]

        def xchunk_cols(slot):
            return slice(slot * FIRST * P, (slot + 1) * FIRST * P)

        def context_of(t):
            first = 2 + CTX_PER_TILE * (t - FIRST - 1)
            return range(first, min(first + CTX_PER_TILE, CTX_CHUNKS))

        block = stack.enter_context(nc.Block())

        @block.sync
        def _(sp):
            def load_mask(k, s):
                sp.dma_start(cols(c_raw, s).bitcast(I32), maskT[ds(k * P, P), :]).then_inc(mask_loaded[s], 16)

            def load_weights(k, s):
                sp.dma_start(cols(w_stage, k), wT[ds(k * P, P), :]).then_inc(w_loaded[s], 16)

            def load_xchunk(k, s):
                sp.dma_start(t_raw[:, xchunk_cols(s)], xT_first[ds(k * P, P), :]).then_inc(xchunk_loaded[s], 16)

            halves = [slice(n * HALF, (n + 1) * HALF) for n in range(NHALF)]
            for n in range(NHALF):
                sp.dma_start(c_raw[:, halves[n]].bitcast(I32), maskT[0:P, halves[n]]).then_inc(first_mask_loaded[n], 16)
            for n in range(NHALF):
                sp.dma_start(w_stage[:, halves[n]], wT[0:P, halves[n]]).then_inc(first_w_loaded[n], 16)
                if n == 0:
                    load_xchunk(0, 0)
            load_mask(1, 1)
            load_weights(1, 1)
            load_xchunk(1, 1)
            sp.dma_start(const_sb[:], consts).then_inc(consts_loaded, 16)
            sp.dma_start(par[:], qparams.partition_broadcast(P)).then_inc(params_loaded, 16)
            with sp.Fori(1, KC // 2) as j:
                for s in range(2):
                    k = 2 * j + s
                    sp.wait_ge(c_raw_read, k - 1)
                    load_mask(k, s)
                    sp.wait_ge(w_masked, k - 1)
                    load_weights(k, s)
                    sp.wait_ge(xchunk_lo, k - 1)
                    load_xchunk(k, s)

            def load_xT(t):
                sp.dma_start(cols(t_raw, t % 2),
                             xT_rest[(t - FIRST) * P:(t - FIRST + 1) * P, :]).then_inc(xT_loaded[t % 2], 16)

            def load_rows(t, loaded):
                sp.dma_start(cols(resid, t), x_rows[t * P:(t + 1) * P, :]).then_inc(loaded, 16)

            def load_context(c):
                sp.wait_ge(c_raw_read, KC + c - 1)
                sp.dma_start(cols(c_raw, c % 2), ctx[c * P:(c + 1) * P, :]).then_inc(ctx_loaded[c % 2], 16)

            load_xT(FIRST)
            for t in range(FIRST):
                load_rows(t, first_rows_loaded[t])
            load_context(0)
            load_context(1)
            sp.wait_ge(xchunk_lo, KC)
            load_xT(FIRST + 1)
            for t in (FIRST, FIRST + 1):
                load_rows(t, rows_loaded[t % 2])
            for t in range(FIRST + 1, TILES):
                if t + 1 < TILES:
                    sp.wait_ge(xT_lo, t - FIRST)
                    load_xT(t + 1)
                if t > FIRST + 1:
                    sp.wait_ge(acc_read, t - 1)
                    load_rows(t, rows_loaded[t % 2])
                for c in context_of(t):
                    load_context(c)

            def load_base(k, s, reuse=True):
                if reuse:
                    sp.wait_ge(w_lo, KC + k - 1)
                sp.dma_start(cols(w_raw, s), baseT[ds(k * P, P), :]).then_inc(base_loaded[s], 16)

            load_base(0, 0, False)
            load_base(1, 1, False)
            sp.wait_ge(c_raw_read, KC + BATCHES * KC)
            sp.dma_start(c_raw[:, 0:KC * AGW], agT).then_inc(ag_loaded, 16)
            sp.dma_start(bias_row[:], base_b.partition_broadcast(P)).then_inc(bias_loaded, 16)
            with sp.Fori(1, KC // 2) as j:
                for s in range(2):
                    load_base(2 * j + s, s)
            sp.wait_ge(w_lo, 2 * KC - 1)
            sp.dma_start(cols(w_raw, 0), lbT).then_inc(lb_loaded, 16)

            with sp.Fori(0, TILES - 1) as t:
                sp.wait_ge(x3_ready, t + 1)
                sp.dma_start(out[ds(t * P, P), :], cols(resid, t)).then_inc(out_stored, 16)
            sp.wait_ge(x3_ready, TILES + 1)
            for half in halves:
                last_rows = cols(resid, TILES - 1)[:, half]
                sp.dma_start(out[(TILES - 1) * P:, half], last_rows).then_inc(out_stored, 16)
            sp.wait_ge(out_stored, 16 * (TILES + 1))

        @block.vector
        def _(dve):
            def row_half_stats(n, row):
                dve.bn_stats(bn[:, 6 * n:6 * n + 6], row).then_inc(stat_step, 1)

            def row_stats(g):
                dve.drain()
                dve.bn_aggr(mean_var[:, 2 * g:2 * g + 2], bn[:]).then_inc(stat_step, 1)

            def row_params(group, tiles_done, width, rstd, nmr):
                base = group * LN_STEPS
                mean, var = (mean_var[:, 0:2 * width].rearrange("p (g c) -> p c g", c=2)[:, c, :] for c in range(2))
                v, minus_half_v, seed, second, third, t = (newton[:, TPB * i:TPB * i + width] for i in range(6))
                dve.wait_ge(stat_step, tiles_done * STAT_STEPS)
                dve.tensor_scalar(v, var, EPS, None, ALU.add).then_inc(ln_step, 1)
                dve.tensor_scalar(minus_half_v, var, EPS, -0.5, ALU.add, ALU.mult).then_inc(ln_step, 1)
                dve.wait_ge(ln_step, base + 1)
                dve.tensor_scalar(seed.bitcast(I32), v.bitcast(I32), -0.5, RSQRT_MAGIC,
                                  ALU.mult, ALU.add).then_inc(ln_step, 1)
                r = seed
                for n, new in enumerate((second, third, rstd)):
                    dve.wait_ge(ln_step, base + 3 + 3 * n)
                    dve.tensor_tensor(t, r, r, ALU.mult).then_inc(ln_step, 1)
                    dve.wait_ge(ln_step, base + 4 + 3 * n)
                    dve.tensor_tensor(t, t, minus_half_v, ALU.mult).then_inc(ln_step, 1)
                    dve.wait_ge(ln_step, base + 5 + 3 * n)
                    dve.scalar_tensor_tensor(new, t, 1.5, r, ALU.add, ALU.mult).then_inc(ln_step, 1)
                    r = new
                dve.wait_ge(ln_step, base + 12)
                dve.scalar_tensor_tensor(nmr, mean, -1.0, rstd, ALU.mult, ALU.mult).then_inc(ln_step, 1)

            def last_params(tile):
                base = tile * LN3_STEPS
                mean, var = mean_var[:, 0:1], mean_var[:, 1:2]
                v, minus_half_v, seed, second, third, t = (newton[:, i:i + 1] for i in range(6))
                dve.wait_ge(stat_step, (2 * TILES + tile + 1) * STAT_STEPS)
                dve.tensor_scalar(v, var, EPS, None, ALU.add).then_inc(ln3_step, 1)
                dve.tensor_scalar(minus_half_v, var, EPS, -0.5, ALU.add, ALU.mult).then_inc(ln3_step, 1)
                dve.wait_ge(ln3_step, base + 1)
                dve.tensor_scalar(seed.bitcast(I32), v.bitcast(I32), -0.5, RSQRT_MAGIC,
                                  ALU.mult, ALU.add).then_inc(ln3_step, 1)
                r = seed
                for n, new in enumerate((second, third, ln3_par[:, 0:1])):
                    dve.wait_ge(ln3_step, base + 3 + 2 * n)
                    dve.scalar_tensor_tensor(t, r, minus_half_v, r, ALU.mult, ALU.mult).then_inc(ln3_step, 1)
                    dve.wait_ge(ln3_step, base + 4 + 2 * n)
                    dve.scalar_tensor_tensor(new, t, 1.5, r, ALU.add, ALU.mult).then_inc(ln3_step, 1)
                    r = new
                dve.wait_ge(ln3_step, base + 9)
                dve.scalar_tensor_tensor(ln3_par[:, 1:2], mean, -1.0, r, ALU.mult, ALU.mult).then_inc(ln3_step, 1)

            def blocks_of(columns):
                return columns.rearrange("p (b c) -> p b c", c=BLK)

            def sum_rows(mask, first, summed):
                cells = blocks_of(mask.bitcast(I32))
                dve.tensor_reduce(row_sums[:, first:first + cells.shape[1]], cells, AX_X, ALU.add).then_inc(summed, 1)

            def sum_blocks(k):
                dve.wait_ge(c_raw_read, k + 1)
                dve.transpose(row_sums_T[:], row_sums[:]).then_inc(mask_step, 1)
                dve.wait_ge(mask_step, MASK_STEPS * k + 1)
                dve.tensor_reduce(block_sum[:], row_sums_T[:], AX_X, ALU.add).then_inc(mask_step, 1)
                dve.wait_ge(mask_step, MASK_STEPS * k + 2)
                dve.transpose(block_sums[:], block_sum[:].to_broadcast([P, NBLK])).then_inc(mask_step, 1)

            def mask_weights(weights, k, first, done):
                w = blocks_of(weights)
                blocks = w.shape[1]
                sums = block_sums[:, first:first + blocks].unsqueeze(2).to_broadcast([P, blocks, BLK])
                dve.wait_ge(mask_step, MASK_STEPS * (k + 1))
                dve.scalar_tensor_tensor(w, sums, 0.0, w, ALU.is_gt, ALU.mult).then_inc(done, 1)

            def mask_chunk(k, s, loads):
                dve.wait_ge(mask_loaded[s], 16 * loads)
                sum_rows(cols(c_raw, s), 0, c_raw_read)
                sum_blocks(k)
                dve.wait_ge(w_loaded[s], 16 * loads)
                mask_weights(cols(w_stage, k), k, 0, w_masked)

            halves = [slice(n * HALF, (n + 1) * HALF) for n in range(NHALF)]
            for n, summed in enumerate((half_summed, c_raw_read)):
                dve.wait_ge(first_mask_loaded[n], 16)
                sum_rows(c_raw[:, halves[n]], n * HALF // BLK, summed)
            dve.wait_ge(half_summed, 1)
            sum_blocks(0)
            for n, masked in enumerate((half_masked, w_masked)):
                dve.wait_ge(first_w_loaded[n], 16)
                mask_weights(w_stage[:, halves[n]], 0, n * HALF // BLK, masked)
            mask_chunk(1, 1, 1)
            with dve.Fori(1, KC // 2) as j:
                mask_chunk(2 * j, 0, j)
                mask_chunk(2 * j + 1, 1, j + 1)

            dve.wait_ge(params_loaded, 16)
            dve.reciprocal(r12, s12).then_inc(par_step, 1)
            dve.tensor_copy(par_u8[:, 0:2], z12).then_inc(par_step, 1)
            dve.tensor_tensor(ss, par[:, 0:1], par[:, 1:2], ALU.mult).then_inc(par_step, 1)
            dve.wait_ge(par_step, 3)
            dve.tensor_copy(zi12, par_u8[:, 0:2]).then_inc(par_step, 1)
            dve.wait_ge(par_step, 4)
            dve.tensor_scalar(neg_zi12, zi12, -1.0, None, ALU.mult).then_inc(par_step, 1)
            dve.tensor_tensor(zf12, z12, zi12, ALU.subtract).then_inc(par_step, 1)
            dve.wait_ge(par_step, 6)
            dve.scalar_tensor_tensor(col_w, zf1, -1.0, ss, ALU.mult, ALU.mult).then_inc(par_step, 1)
            dve.scalar_tensor_tensor(row_w, zf2, -1.0, ss, ALU.mult, ALU.mult).then_inc(par_step, 1)
            dve.wait_ge(par_step, 8)
            dve.scalar_tensor_tensor(row_c, row_w, -float(D), zf1, ALU.mult, ALU.mult).then_inc(par_step, 1)
            dve.wait_ge(par_step, 9)
            dve.memset(ctx_u16[:, 0:1], 0.0).then_inc(ctx_u16_free, 2)
            dve.memset(ones_f16[:], 1.0).then_inc(par_ready, 1)
            dve.wait_ge(consts_loaded, 16)
            dve.tensor_copy(ident_bf[:], ident).then_inc(consts_ready, 1)

            def add_rows1(t, pair):
                dve.wait_ge(product_done, t + 1)
                dve.tensor_tensor(cols(resid, t), acc2(pair), cols(resid, t), ALU.add).then_inc(acc_read, 1)

            def tile_stats(t, g):
                dve.drain()
                for n in range(NHALF):
                    row_half_stats(n, resid[:, ds(t * D + n * HALF, HALF)])
                row_stats(g)

            def quant_params(c):
                row_params(c, 2 * c + 2, 2, rstd1, nmr1)
                dve.wait_ge(ln_step, (c + 1) * LN_STEPS)
                dve.tensor_scalar(q_scale, rstd1, r1, None, ALU.mult).then_inc(q_par, 1)
                dve.tensor_scalar(q_bias, nmr1, r1, z1, ALU.mult, ALU.add).then_inc(q_par, 1)

            def apply1(c):
                dve.wait_ge(q_rows_done, 2 * c + 2)
                dve.tensor_scalar(row_corr, row_sum, row_w, row_c, ALU.mult, ALU.add).then_inc(apply_step, 1)
                dve.wait_ge(apply_step, 2 * c + 1)
                dve.tensor_tensor(shift1, row_corr, nmr1, ALU.add).then_inc(apply_step, 1)
                dve.wait_ge(apply_step, 2 * c + 2)
                for g in range(2):
                    dve.tensor_scalar(cols(resid, 2 * c + g), cols(resid, 2 * c + g), rstd1[:, g:g + 1],
                                      shift1[:, g:g + 1], ALU.mult, ALU.add).then_inc(x1_ready, 1)

            def context_chunks(pair):
                for c in pair:
                    dve.wait_ge(c_raw_read, KC + c + 1)
                    dve.tensor_scalar(cols(ctx_q, c), cols(ctx_u16, c % 2), Q_MAX, zi2,
                                      ALU.min, ALU.subtract).then_inc(ctx_u16_free, 1)
                for c in pair:
                    b, nth = divmod(c, KC)
                    total = cols(ctx_sum, b)
                    if nth:
                        dve.wait_ge(ctx_u16_free, 2 + c + 1)
                        if nth > 1:
                            dve.wait_ge(ctx_sum_done, (KC - 1) * b + nth - 1)
                        dve.tensor_tensor(total, cols(ctx_q, c - 1) if nth == 1 else total,
                                          cols(ctx_q, c), ALU.add).then_inc(ctx_sum_done, 1)

            for t in range(2):
                dve.wait_ge(first_rows_loaded[t], 16)
                add_rows1(t, t)
            for t in range(2):
                tile_stats(t, t)
            quant_params(0)
            dve.wait_ge(first_rows_loaded[2], 16)
            add_rows1(2, 2)
            tile_stats(2, 0)
            dve.wait_ge(w_lo, KC)
            context_chunks((0, 1))
            apply1(0)
            for t in range(FIRST + 1, TILES):
                dve.wait_ge(rows_loaded[(t - 1) % 2], 16 * ((t - FIRST + 1) // 2))
                add_rows1(t - 1, PAIR[(t - 1) % 2])
                tile_stats(t - 1, (t - 1) % 2)
                chunks = context_of(t)
                context_chunks(chunks[:2])
                if t % 2 == 0:
                    quant_params(t // 2 - 1)
                context_chunks(chunks[2:])
                if t == 5:
                    apply1(1)
            dve.wait_ge(rows_loaded[1], 16 * 3)
            add_rows1(TILES - 1, PAIR[1])
            tile_stats(TILES - 1, 1)
            apply1(2)
            quant_params(3)

            def add_rows2(t, s):
                dve.wait_ge(resid_added, t + 1)
                dve.wait_ge(product_done, TILES + t + 1)
                dve.scalar_tensor_tensor(cols(resid, t), acc2(PAIR[s]), ss, cols(resid, t),
                                         ALU.mult, ALU.add).then_inc(acc_read, 1)

            def rows2(t, s, g):
                add_rows2(t, s)
                tile_stats(t, g)

            def split_x2T(t, s):
                for n in range(NHALF):
                    dve.wait_ge(x2T_hi, NHALF * t + n + 1)
                    dve.tensor_tensor(t_l[:, s * D + n * HALF:s * D + (n + 1) * HALF], acc(X2T_PAIR, n),
                                      t_h[:, s * D + n * HALF:s * D + (n + 1) * HALF].bitcast(F32),
                                      ALU.subtract).then_inc(x2T_lo, 1)

            def batch_params(b):
                row_params(PAIR_GROUPS + b, TILES + (b + 1) * TPB, TPB,
                           rstd2[:, b * TPB:(b + 1) * TPB], nmr2[:, b * TPB:(b + 1) * TPB])

            rows2(0, 0, 0)
            rows2(1, 1, 1)
            apply1(3)
            rows2(2, 0, 2)
            rows2(3, 1, 3)
            batch_params(0)
            for t in range(TPB, TILES - 2):
                rows2(t, t % 2, t - TPB)
            add_rows2(TILES - 2, 0)
            split_x2T(0, 0)
            tile_stats(TILES - 2, TPB - 2)
            rows2(TILES - 1, 1, TPB - 1)

            def route_tokens(t):
                base = t * GATE_STEPS
                dve.wait_ge(logits_done, t + 1)
                dve.tensor_copy(low_logits[:], bank(LOGITS, AGW)).then_inc(gate_step, 1)
                dve.wait_ge(gate_step, base + 1)
                dve.tensor_tensor(low_logits[:], low_logits[:], bank(LOGITS, AGW, at=AGW), ALU.add).then_inc(gate_step, 1)
                dve.drain()
                dve.max(top8[:], low_logits[:, ER:]).then_inc(gate_step, 1)
                dve.wait_ge(gate_step, base + 3)
                dve.tensor_tensor(gate[:, 0:1], top8[:, 1:2], top8[:, 0:1], ALU.subtract).then_inc(gate_diff, 1)
                dve.max_index(top_i[:], top8[:], low_logits[:, ER:]).then_inc(gate_step, 1)
                dve.wait_ge(gate_step, base + 4)
                dve.tensor_copy(gate[:, 2:4], top_i[:, 0:2]).then_inc(gate_step, 1)
                dve.wait_ge(gate_exp, t + 1)
                dve.tensor_scalar(gate[:, 4:5], gate[:, 1:2], 1.0, None, ALU.add).then_inc(gate_step, 1)
                dve.wait_ge(gate_step, base + 6)
                dve.reciprocal(gate[:, 5:6], gate[:, 4:5]).then_inc(gate_step, 1)
                dve.wait_ge(gate_step, base + 7)
                dve.tensor_tensor(gate[:, 6:7], gate[:, 1:2], gate[:, 5:6], ALU.mult).then_inc(gate_step, 1)
                dve.tensor_scalar(route[:, 0:EXPERTS], iota, gate[:, 2:3], gate[:, 5:6],
                                  ALU.is_equal, ALU.mult).then_inc(gate_step, 1)
                dve.wait_ge(gate_step, base + 8)
                dve.tensor_scalar(route[:, EXPERTS:2 * EXPERTS], iota, gate[:, 3:4], gate[:, 6:7],
                                  ALU.is_equal, ALU.mult).then_inc(gate_step, 1)
                dve.wait_ge(gate_step, base + 10)
                dve.tensor_tensor(route[:, 2 * EXPERTS:], route[:, 0:EXPERTS], route[:, EXPERTS:2 * EXPERTS],
                                  ALU.add).then_inc(gate_step, 1)
                dve.wait_ge(gate_step, base + 11)
                dve.scalar_tensor_tensor(low_w[:].rearrange("p (e r) -> p e r", r=RANK),
                                         low_logits[:, 0:ER].rearrange("p (e r) -> p e r", r=RANK), SCALING,
                                         route[:, 2 * EXPERTS:].unsqueeze(2).to_broadcast([P, EXPERTS, RANK]),
                                         ALU.mult, ALU.mult).then_inc(low_ready, 1)

            def mixture_rows(t, s, more=True, first=False):
                route_tokens(t)
                if first:
                    batch_params(1)
                dve.wait_ge(lowT_hi, t + 1)
                dve.tensor_tensor(lowT_l[:], bank(LOWT, P), lowT_h[:].bitcast(F32), ALU.subtract).then_inc(lowT_lo, 1)
                if more:
                    split_x2T(t + 1, 1 - s)
                halves = [resid[:, ds(t * D + n * HALF, HALF)] for n in range(NHALF)]
                dve.wait_ge(resid_added, TILES + t + 1)
                dve.wait_ge(half_done, t + 1)
                dve.tensor_tensor(halves[0], acc(PAIR[s], 0), halves[0], ALU.add)
                dve.drain()
                row_half_stats(0, halves[0])
                dve.wait_ge(product_done, 2 * TILES + t + 1)
                dve.tensor_tensor(halves[1], acc(PAIR[s], 1), halves[1], ALU.add).then_inc(acc_read, 1)
                dve.drain()
                row_half_stats(1, halves[1])
                row_stats(0)
                last_params(t)
                dve.wait_ge(ln3_step, (t + 1) * LN3_STEPS)
                part = cols(resid, t) if more else halves[0]
                dve.tensor_scalar(part, part, ln3_par[:, 0:1], ln3_par[:, 1:2],
                                  ALU.mult, ALU.add).then_inc(x3_ready, 1)

            mixture_rows(0, 0, first=True)
            mixture_rows(1, 1)
            with dve.Fori(1, TILES // 2 - 1) as j:
                for s in range(2):
                    mixture_rows(2 * j + s, s)
            mixture_rows(TILES - 2, 0)
            mixture_rows(TILES - 1, 1, more=False)

        @block.scalar
        def _(act):
            def round_xchunk(s):
                nc.scalar.activation(t_h[:, xchunk_cols(s)], t_raw[:, xchunk_cols(s)], ACT.Copy).then_inc(xchunk_hi, 1)

            def round_weights(k):
                act.wait_ge(w_masked, k + 1)
                nc.scalar.activation(cols(w_h, k), cols(w_stage, k), ACT.Copy).then_inc(w_hi, 1)

            act.wait_ge(xchunk_loaded[0], 16)
            round_xchunk(0)
            for n, (masked, high) in enumerate(((half_masked, half_hi), (w_masked, w_hi))):
                half = slice(n * HALF, (n + 1) * HALF)
                act.wait_ge(masked, 1)
                nc.scalar.activation(w_h[:, half], w_stage[:, half], ACT.Copy).then_inc(high, 1)
            act.wait_ge(xchunk_loaded[1], 16)
            round_xchunk(1)
            round_weights(1)
            with act.Fori(1, KC // 2) as j:
                for s in range(2):
                    k = 2 * j + s
                    act.wait_ge(xchunk_loaded[s], 16 * (j + 1))
                    act.wait_ge(chunk_done, k - 1)
                    round_xchunk(s)
                    round_weights(k)

            def round_xT(t):
                act.wait_ge(xT_loaded[t % 2], 16 * ((t - FIRST) // 2 + 1))
                if t > FIRST:
                    act.wait_ge(product_done, t - 1)
                nc.scalar.activation(cols(t_h, t % 2), cols(t_raw, t % 2), ACT.Copy).then_inc(xT_hi, 1)

            round_xT(FIRST)
            round_xT(FIRST + 1)

            def quantise_rows(t, s):
                nc.scalar.activation(cols(q_u8, s), cols(resid, t), ACT.Identity, bias=q_bias[:, s:s + 1],
                                     scale=q_scale[:, s:s + 1]).then_inc(q_done, 1)
                act.wait_ge(q_done, t + 1)
                nc.scalar.activation(cols(q_rows, t), cols(q_u8, s), ACT.Identity, bias=neg_zi1,
                                     accum_out=row_sum[:, s:s + 1]).then_inc(q_rows_done, 1)

            def quantise_pair(c):
                act.wait_ge(q_par, 2 * c + 2)
                for s in range(2):
                    quantise_rows(2 * c + s, s)

            def quantise_context(pair):
                for c in pair:
                    act.wait_ge(ctx_loaded[c % 2], 16 * (c // 2 + 1))
                    act.wait_ge(ctx_u16_free, c + 1)
                    nc.scalar.activation(cols(ctx_u16, c % 2), cols(c_raw, c % 2), ACT.Identity, bias=z2,
                                         scale=r2).then_inc(c_raw_read, 1)

            act.wait_ge(par_ready, 1)
            quantise_context((0, 1))
            quantise_pair(0)
            for t in range(FIRST + 1, TILES - 1):
                round_xT(t + 1)
                quantise_context(context_of(t))
                if t == 4:
                    quantise_pair(1)

            def column_correction(b):
                act.wait_ge(colsum_done, b + 1)
                act.wait_ge(xT_lo, TILES - FIRST - 1 + b)
                nc.scalar.activation(cols(t_raw, b), acc2(COLSUM), ACT.Copy, scale=col_w).then_inc(corr_ready, 1)

            def copy_qT(t):
                act.wait_ge(q_transposed, t + 1)
                if t >= 2:
                    act.wait_ge(product_done, TILES + t - 1)
                nc.scalar.activation(cols(qT, t % 2), acc2(QT_PAIR[t % 2] if t else QT_PAIR[1]),
                                     ACT.Copy).then_inc(qT_ready, 1)

            def round_base(k):
                if k == 0:
                    act.wait_ge(product_done, TILES)
                act.wait_ge(base_loaded[k % 2], 16 * (k // 2 + 1))
                nc.scalar.activation(cols(w_h, k), cols(w_raw, k % 2), ACT.Copy).then_inc(w_hi, 1)

            def normalise2(t, s):
                nc.scalar.activation(cols(t_raw, s), cols(resid, t), ACT.Identity, bias=cols(nmr2, t, 1),
                                     scale=cols(rstd2, t, 1)).then_inc(x2_rows, 1)

            def round_x2T(t, s):
                act.wait_ge(product_done, 2 * TILES + t - 1)
                for n in range(NHALF):
                    act.wait_ge(x2_transposed, NHALF * t + n + 1)
                    nc.scalar.activation(t_h[:, s * D + n * HALF:s * D + (n + 1) * HALF], acc(X2T_PAIR, n),
                                         ACT.Copy).then_inc(x2T_hi, 1)

            copy_qT(0)
            column_correction(0)
            quantise_context(context_of(TILES - 1))
            quantise_pair(2)
            copy_qT(1)
            column_correction(1)
            round_base(0)
            round_base(1)
            copy_qT(2)
            act.wait_ge(q_par, 2 * (TILES // 2))
            quantise_rows(TILES - 2, 0)
            copy_qT(3)
            quantise_rows(TILES - 1, 1)
            for k in range(2, KC - 2):
                if k > 2:
                    copy_qT(k + 1)
                round_base(k)
            act.wait_ge(ln_step, (PAIR_GROUPS + 1) * LN_STEPS)
            act.wait_ge(resid_added, TPB)
            normalise2(0, 0)
            copy_qT(TILES - 1)
            act.wait_ge(q_transposed, TILES)
            act.wait_ge(ag_loaded, 16)
            nc.scalar.activation(ag_high, ag_raw, ACT.Copy).then_inc(small_hi, 1)
            round_x2T(0, 0)
            round_base(KC - 2)
            round_base(KC - 1)
            act.wait_ge(resid_added, TILES)
            normalise2(1, 1)
            act.wait_ge(lb_loaded, 16)
            nc.scalar.activation(lb_h[:], cols(w_raw, 0), ACT.Copy).then_inc(small_hi, 1)

            def mixture_tile(t, s, left):
                act.wait_ge(gate_diff, t + 1)
                nc.scalar.activation(gate[:, 1:2], gate[:, 0:1], ACT.Exp).then_inc(gate_exp, 1)
                act.wait_ge(low_transposed, t + 1)
                nc.scalar.activation(lowT_h[:], bank(LOWT, P), ACT.Copy).then_inc(lowT_hi, 1)
                if left >= 1:
                    round_x2T(t + 1, 1 - s)
                if left >= 2:
                    act.wait_ge(ln_step, (PAIR_GROUPS + 2) * LN_STEPS)
                    act.wait_ge(resid_added, TILES + t + 1)
                    normalise2(t + 2, s)

            with act.Fori(0, TILES // 2 - 1) as j:
                for s in range(2):
                    mixture_tile(2 * j + s, s, 2)
            mixture_tile(TILES - 2, 0, 1)
            mixture_tile(TILES - 1, 1, 0)
            act.wait_ge(ln3_step, TILES * LN3_STEPS)
            half = resid[:, TILES * D - HALF:TILES * D]
            nc.scalar.activation(half, half, ACT.Identity, bias=ln3_par[:, 1:2],
                                 scale=ln3_par[:, 0:1]).then_inc(x3_ready, 1)

        @block.gpsimd
        def _(pool):
            def low_part(out, raw, high):
                return pool.tensor_tensor(out, raw, high.bitcast(F32), ALU.subtract)

            def split_weights(nth, k, raw):
                pool.wait_ge(w_hi, nth + 1)
                low_part(cols(w_l, k), raw, cols(w_h, k)).then_inc(w_lo, 1)

            def split_xchunk(k, s):
                pool.wait_ge(xchunk_hi, k + 1)
                low_part(t_l[:, xchunk_cols(s)], t_raw[:, xchunk_cols(s)], t_h[:, xchunk_cols(s)]).then_inc(xchunk_lo, 1)

            split_xchunk(0, 0)
            for n, (high, low) in enumerate(((half_hi, half_lo), (w_hi, w_lo))):
                half = slice(n * HALF, (n + 1) * HALF)
                pool.wait_ge(high, 1)
                low_part(w_l[:, half], w_stage[:, half], w_h[:, half]).then_inc(low, 1)
            split_xchunk(1, 1)
            split_weights(1, 1, cols(w_stage, 1))
            with pool.Fori(1, KC // 2) as j:
                for s in range(2):
                    k = 2 * j + s
                    split_xchunk(k, s)
                    split_weights(k, k, cols(w_stage, k))

            pool.wait_ge(xT_hi, 1)
            low_part(cols(t_l, 1), cols(t_raw, 1), cols(t_h, 1)).then_inc(xT_lo, 1)
            with pool.Fori(2, TILES // 2) as j:
                for s in range(2):
                    t = 2 * j + s
                    pool.wait_ge(xT_hi, t - FIRST + 1)
                    low_part(cols(t_l, s), cols(t_raw, s), cols(t_h, s)).then_inc(xT_lo, 1)

            def add_correction(t, b):
                pool.wait_ge(x1_ready, t + 1)
                pool.tensor_tensor(cols(resid, t), cols(resid, t), cols(t_raw, b), ALU.add).then_inc(resid_added, 1)

            pool.wait_ge(corr_ready, 1)
            with pool.Fori(0, TPB) as t:
                add_correction(t, 0)
            pool.wait_ge(corr_ready, 2)
            with pool.Fori(0, TPB // 2) as j:
                for s in range(2):
                    k = 2 * j + s
                    split_weights(KC + k, k, cols(w_raw, s))
                    add_correction(TPB + k, 1)
            split_weights(KC + TPB, TPB, cols(w_raw, 0))
            split_weights(KC + TPB + 1, TPB + 1, cols(w_raw, 1))
            pool.wait_ge(small_hi, 1)
            low_part(ag_low, ag_raw, ag_high).then_inc(small_lo, 1)
            split_weights(KC + TPB + 2, TPB + 2, cols(w_raw, 0))
            split_weights(KC + TPB + 3, TPB + 3, cols(w_raw, 1))
            pool.wait_ge(small_hi, 2)
            low_part(lb_l[:], cols(w_raw, 0), lb_h[:]).then_inc(small_lo, 1)

            pool.wait_ge(bias_loaded, 16)
            with pool.Fori(0, TILES // 2) as j:
                for s in range(2):
                    t = 2 * j + s
                    pool.wait_ge(x2_rows, t + 1)
                    pool.tensor_tensor(cols(resid, t), cols(t_raw, s), bias_row[:], ALU.add).then_inc(resid_added, 1)

        @block.tensor
        def _(pe):
            def w_half(tensor, k, n):
                return tensor[:, ds(k * D + n * HALF, HALF)]

            def chunk_cols(s, t):
                return slice((s * FIRST + t) * P, (s * FIRST + t + 1) * P)

            def chunk_products(k, s, stop=False):
                pe.wait_ge(w_hi, k + 1)
                for t in range(FIRST):
                    for n in range(NHALF):
                        pe.matmul(acc(t, n), t_h[:, chunk_cols(s, t)], w_half(w_h, k, n), start=False, stop=False)
                pe.wait_ge(xchunk_lo, k + 1)
                pe.wait_ge(w_lo, k + 1)
                for t in range(FIRST):
                    for n in range(NHALF):
                        pe.matmul(acc(t, n), t_l[:, chunk_cols(s, t)], w_half(w_h, k, n), start=False, stop=False)
                        last = pe.matmul(acc(t, n), t_h[:, chunk_cols(s, t)], w_half(w_l, k, n),
                                         start=False, stop=stop)
                    if stop:
                        last.then_inc(product_done, 1)
                if not stop:
                    last.then_inc(chunk_done, 1)

            for n, high in enumerate((half_hi, w_hi)):
                pe.wait_ge(high, 1)
                for t in range(FIRST):
                    pe.matmul(acc(t, n), t_h[:, chunk_cols(0, t)], w_half(w_h, 0, n), start=True, stop=False)
            pe.wait_ge(xchunk_lo, 1)
            for n, low in enumerate((half_lo, w_lo)):
                pe.wait_ge(low, 1)
                for t in range(FIRST):
                    pe.matmul(acc(t, n), t_l[:, chunk_cols(0, t)], w_half(w_h, 0, n), start=False, stop=False)
                    last = pe.matmul(acc(t, n), t_h[:, chunk_cols(0, t)], w_half(w_l, 0, n), start=False, stop=False)
            last.then_inc(chunk_done, 1)
            chunk_products(1, 1)
            with pe.Fori(1, KC // 2 - 1) as j:
                for s in range(2):
                    chunk_products(2 * j + s, s)
            chunk_products(KC - 2, 0)
            chunk_products(KC - 1, 1, stop=True)

            def split_product(s, n, chunks, stop, weights_due=None):
                last = None
                for k in chunks:
                    if k == KC - 2 and weights_due:
                        pe.wait_ge(w_lo, weights_due)
                    hi = t_h[:, s * D + k * P:s * D + (k + 1) * P]
                    lo = t_l[:, s * D + k * P:s * D + (k + 1) * P]
                    pe.matmul(acc(PAIR[s], n), hi, w_half(w_h, k, n), start=(k == 0), stop=False)
                    pe.matmul(acc(PAIR[s], n), hi, w_half(w_l, k, n), start=False, stop=False)
                    last = pe.matmul(acc(PAIR[s], n), lo, w_half(w_h, k, n), start=False, stop=(stop and k == KC - 1))
                return last

            def stage1_tile(t, s, reads):
                pe.wait_ge(acc_read, reads)
                pe.wait_ge(xT_hi, t - FIRST + 1)
                pe.wait_ge(xT_lo, t - FIRST + 1)
                for n in range(NHALF):
                    last = split_product(s, n, range(KC), True)
                last.then_inc(product_done, 1)

            with pe.Fori(1, TILES // 2 - 1) as j:
                stage1_tile(2 * j + 1, 1, 3 * j - 2)
                stage1_tile(2 * j + 2, 0, 2 * j + 1)

            def column_sums(b):
                pe.wait_ge(ctx_sum_done, (KC - 1) * (b + 1))
                for n in range(NHALF):
                    last = pe.matmul(acc(COLSUM, n), ones_f16[:], ctx_sum[:, b * D + n * HALF:b * D + (n + 1) * HALF],
                                     start=True, stop=True)
                last.then_inc(colsum_done, 1)

            def transpose_q(t, pair):
                pe.wait_ge(q_rows_done, t + 1)
                for k in range(KC):
                    last = pe.matmul(ps[:, pair * D + k * P:pair * D + (k + 1) * P],
                                     q_rows[:, ds(t * D + k * P, P)], ident_bf[:], start=True, stop=True,
                                     skip_group_check=True)
                last.then_inc(q_transposed, 1)

            def stage2_product(t, s, b):
                pe.wait_ge(qT_ready, t + 1)
                pe.wait_ge(acc_read, TILES + t - 1)
                for n in range(NHALF):
                    for k in range(KC):
                        last = pe.matmul(acc(PAIR[s], n), qT[:, s * D + k * P:s * D + (k + 1) * P],
                                         w_half(ctx_q, b * KC + k, n), start=(k == 0), stop=(k == KC - 1))
                last.then_inc(product_done, 1)

            pe.wait_ge(par_ready, 1)
            pe.wait_ge(consts_ready, 1)
            transpose_q(0, QT_PAIR[1])
            pe.wait_ge(acc_read, FIRST)
            column_sums(0)
            stage1_tile(TILES - 1, 1, TILES - 2)
            pe.wait_ge(qT_ready, 1)
            transpose_q(1, QT_PAIR[1])
            pe.wait_ge(corr_ready, 1)
            column_sums(1)
            with pe.Fori(0, TPB // 2) as j:
                stage2_product(2 * j, 0, 0)
                pe.wait_ge(corr_ready, 2)
                transpose_q(2 * j + 2, QT_PAIR[0])
                stage2_product(2 * j + 1, 1, 0)
                transpose_q(2 * j + 3, QT_PAIR[1])
            stage2_product(4, 0, 1)
            transpose_q(6, QT_PAIR[0])
            stage2_product(5, 1, 1)
            transpose_q(7, QT_PAIR[1])
            stage2_product(6, 0, 1)

            def transpose_x2(t, s):
                pe.wait_ge(x2_rows, t + 1)
                for n in range(NHALF):
                    for k in range(n * KC // 2, (n + 1) * KC // 2):
                        last = pe.transpose(ps[:, X2T_PAIR * D + k * P:X2T_PAIR * D + (k + 1) * P],
                                            t_raw[:, s * D + k * P:s * D + (k + 1) * P], ident)
                    last.then_inc(x2_transposed, 1)

            def low_and_logits(t, s):
                pe.wait_ge(x2T_hi, NHALF * (t + 1))
                pe.wait_ge(x2T_lo, NHALF * (t + 1))
                for k in range(KC):
                    hi = t_h[:, s * D + k * P:s * D + (k + 1) * P]
                    lo = t_l[:, s * D + k * P:s * D + (k + 1) * P]
                    high_low = ag_hl[:, k * 2 * AGW:(k + 1) * 2 * AGW]
                    pe.matmul(bank(LOGITS, 2 * AGW), hi, high_low, start=(k == 0), stop=False)
                    last = pe.matmul(bank(LOGITS, 2 * AGW), lo, high_low, start=False, stop=(k == KC - 1))
                last.then_inc(logits_done, 1)

            def lora_product(s, n):
                half = slice(n * HALF, (n + 1) * HALF)
                pe.matmul(acc(PAIR[s], n), lowT_h[:], lb_h[:, half], start=False, stop=False)
                pe.matmul(acc(PAIR[s], n), lowT_h[:], lb_l[:, half], start=False, stop=False)
                return pe.matmul(acc(PAIR[s], n), lowT_l[:], lb_h[:, half], start=False, stop=True)

            def stage3_tile(t, s, more=True):
                low_and_logits(t, s)
                pe.wait_ge(w_lo, 2 * KC - 2)
                pe.wait_ge(acc_read, 2 * TILES + t - 1)
                split_product(s, 0, range(KC), False, weights_due=2 * KC)
                if more:
                    transpose_x2(t + 1, 1 - s)
                early = 0 if more else 1
                split_product(s, 1, range(early), False)
                pe.wait_ge(low_ready, t + 1)
                pe.transpose(bank(LOWT, P), low_w[:], ident).then_inc(low_transposed, 1)
                split_product(s, 1, range(early, KC // 2), False)
                pe.wait_ge(lowT_hi, t + 1)
                pe.wait_ge(lowT_lo, t + 1)
                pe.wait_ge(small_lo, 2)
                lora_product(s, 0).then_inc(half_done, 1)
                split_product(s, 1, range(KC // 2, KC), False)
                lora_product(s, 1).then_inc(product_done, 1)

            transpose_x2(0, 0)
            stage2_product(TILES - 1, 1, 1)
            pe.wait_ge(small_lo, 1)
            with pe.Fori(0, TILES // 2 - 1) as j:
                for s in range(2):
                    stage3_tile(2 * j + s, s)
            stage3_tile(TILES - 2, 0)
            stage3_tile(TILES - 1, 1, more=False)


def kernel(**inputs):
    import numpy as np
    import concourse.bacc as bacc
    from concourse.bass_utils import run_bass_kernel_spmd

    def arr(name):
        return np.asarray(inputs[name])

    x_rows = arr("x").reshape(TOK, D)
    consts = np.concatenate([np.eye(P), np.broadcast_to(np.arange(EXPERTS), (P, EXPERTS))], axis=1).astype(np.float32)
    laid_out = {
        "xT_first": x_rows[:FIRST * P].T,
        "xT_rest": x_rows[FIRST * P:].reshape(TILES - FIRST, P, KC, P).transpose(0, 3, 2, 1).reshape(-1, D),
        "x_rows": x_rows,
        "ctx": arr("ctx_4096").reshape(BATCHES * D, D),
        "wT": arr("L0_attn_weight").T,
        "maskT": arr("L0_attn_mask").T,
        "qparams": np.concatenate([arr("L0_xattn_x1_scale"), arr("L0_xattn_x2_scale"),
                                   arr("L0_xattn_x1_zp"), arr("L0_xattn_x2_zp")]),
        "agT": np.concatenate([arr("L0_ffn_lora_A").reshape(ER, D), arr("L0_ffn_gate_w")], axis=0)
                 .T.reshape(KC, P, AGW).transpose(1, 0, 2).reshape(P, KC * AGW),
        "baseT": arr("L0_ffn_base_w").T,
        "base_b": arr("L0_ffn_base_b"),
        "lbT": arr("L0_ffn_lora_B").transpose(0, 2, 1).reshape(ER, D),
        "consts": consts,
    }
    nc = bacc.Bacc("TRN2", target_bir_lowering=False, num_devices=1)
    arrays, args = {}, []
    for name, a in laid_out.items():
        a = np.ascontiguousarray(a)
        arrays[f"in_{name}"] = a
        args.append(nc.dram_tensor(f"in_{name}", a.shape, mybir.dt.from_np(a.dtype), kind="ExternalInput").ap())
    out = nc.dram_tensor("out", (TOK, D), F32, kind="ExternalOutput").ap()
    decoder_layer(nc, *args, out)
    result = run_bass_kernel_spmd(nc, [arrays], core_ids=[0])
    return result.results[0]["out"].reshape(BATCHES, TOK // BATCHES, D)
```
